# Optimizing a Trainium2 kernel written in Bass

```python
import numpy as np
import jax
import jax.numpy as jnp

def _softmax(x, axis=-1):
    return jax.nn.softmax(x, axis=axis)

def _gelu(x):
    return jax.nn.gelu(x, approximate=True)

def _silu(x):
    return jax.nn.silu(x)

def _sigmoid(x):
    return jax.nn.sigmoid(x)

def _layernorm(x, axis=-1, eps=1e-05):
    m = jnp.mean(x, axis=axis, keepdims=True)
    v = jnp.var(x, axis=axis, keepdims=True)
    return (x - m) / jnp.sqrt(v + eps)

def _scatter_add(tgt, idx, src, axis=0):
    return tgt.at[idx].add(src)

def _segment_sum(src, seg, n):
    return jax.ops.segment_sum(src, seg, n)
kernel_name = 'mk_gnn_resnorm_d2_gnn_r32_351ebc'

def setup_inputs(seed: int=0):
    np.random.seed(seed)
    _w = jnp.asarray

    def _rec_inputs():
        import jax
        import jax.numpy as jnp
        _gk = jax.random.key(seed)
        x = -0.000202 + 1 * jax.random.normal(jax.random.fold_in(_gk, 1), (3125, 128), jnp.float32)
        src = jax.random.randint(jax.random.fold_in(_gk, 2), (100000,), 0, 3125, jnp.int32)
        dst = jax.random.randint(jax.random.fold_in(_gk, 3), (100000,), 0, 3125, jnp.int32)
        _o = jnp.argsort(dst, stable=True)
        src = src[_o]
        dst = dst[_o]
        return (x, src, dst)
    x, src, dst = _rec_inputs()

    def _L0_gnn_setup():
        import jax, jax.numpy as jnp
        import numpy as np
        D = 128
        STEPS = 2
        N = 50000
        E = 15625

        def _mlp2(h, W1, b1, W2, b2):
            return jax.nn.relu(h @ W1 + b1) @ W2 + b2
        key = jax.random.key(seed)
        ks = jax.random.split(key, 16)
        s = 1.0 / np.sqrt(2 * D)
        t = 1.0 / np.sqrt(D)
        inp = {'x': jax.random.normal(ks[0], (N, D), dtype=jnp.float32), 'edge_index': jax.random.randint(ks[1], (2, E), 0, N, dtype=jnp.int64), 'msg_W1': jax.random.uniform(ks[2], (2 * D, D), jnp.float32, -s, s), 'msg_b1': jnp.zeros((D,), jnp.float32), 'msg_W2': jax.random.uniform(ks[3], (D, D), jnp.float32, -t, t), 'msg_b2': jnp.zeros((D,), jnp.float32), 'upd_W1': jax.random.uniform(ks[4], (2 * D, D), jnp.float32, -s, s), 'upd_b1': jnp.zeros((D,), jnp.float32), 'upd_W2': jax.random.uniform(ks[5], (D, D), jnp.float32, -t, t), 'upd_b2': jnp.zeros((D,), jnp.float32), 'att_W1': jax.random.uniform(ks[6], (2 * D, D), jnp.float32, -s, s), 'att_b1': jnp.zeros((D,), jnp.float32), 'att_W2': jax.random.uniform(ks[7], (D, 1), jnp.float32, -t, t), 'att_b2': jnp.zeros((1,), jnp.float32), 'glb_W': jax.random.uniform(ks[8], (D, D), jnp.float32, -t, t), 'glb_b': jnp.zeros((D,), jnp.float32)}
        return inp
    _L0_gnn_all = _L0_gnn_setup()
    _L0_gnn_in = {k: v for k, v in _L0_gnn_all.items() if k in ('msg_W1', 'msg_b1', 'msg_W2', 'msg_b2', 'upd_W1', 'upd_b1', 'upd_W2', 'upd_b2', 'att_W1', 'att_b1', 'att_W2', 'att_b2', 'glb_W', 'glb_b')}
    del _L0_gnn_all

    def _L1_gnn_setup():
        import jax, jax.numpy as jnp
        import numpy as np
        N_NODES = 50000
        N_EDGES = 25000
        D_IN = 128
        D_OUT = 128
        key = jax.random.key(seed)
        ks = jax.random.split(key, 12)
        sc_in = 1.0 / np.sqrt(D_IN)
        sc_out = 1.0 / np.sqrt(D_OUT)
        return {'feature': jax.random.normal(ks[0], (N_NODES, D_IN), dtype=jnp.float32), 'Wq': jax.random.uniform(ks[1], (D_IN, D_OUT), jnp.float32, -sc_in, sc_in), 'bq': jax.random.uniform(ks[2], (D_OUT,), jnp.float32, -sc_in, sc_in), 'Wk': jax.random.uniform(ks[3], (D_IN, D_OUT), jnp.float32, -sc_in, sc_in), 'bk': jax.random.uniform(ks[4], (D_OUT,), jnp.float32, -sc_in, sc_in), 'Wv': jax.random.uniform(ks[5], (D_IN, D_OUT), jnp.float32, -sc_in, sc_in), 'bv': jax.random.uniform(ks[6], (D_OUT,), jnp.float32, -sc_in, sc_in), 'Wl': jax.random.uniform(ks[7], (D_OUT, D_OUT), jnp.float32, -sc_out, sc_out), 'bl': jax.random.uniform(ks[8], (D_OUT,), jnp.float32, -sc_out, sc_out), 'src': jax.random.randint(ks[9], (N_EDGES,), 0, N_NODES, dtype=jnp.int32), 'dst': jax.random.randint(ks[10], (N_EDGES,), 0, N_NODES, dtype=jnp.int32)}
    _L1_gnn_all = _L1_gnn_setup()
    _L1_gnn_in = {k: v for k, v in _L1_gnn_all.items() if k in ('Wq', 'bq', 'Wk', 'bk', 'Wv', 'bv', 'Wl', 'bl')}
    del _L1_gnn_all
    return {'x': x, 'src': src, 'dst': dst, 'L0_gnn_msg_W1': _L0_gnn_in['msg_W1'], 'L0_gnn_msg_b1': _L0_gnn_in['msg_b1'], 'L0_gnn_msg_W2': _L0_gnn_in['msg_W2'], 'L0_gnn_msg_b2': _L0_gnn_in['msg_b2'], 'L0_gnn_upd_W1': _L0_gnn_in['upd_W1'], 'L0_gnn_upd_b1': _L0_gnn_in['upd_b1'], 'L0_gnn_upd_W2': _L0_gnn_in['upd_W2'], 'L0_gnn_upd_b2': _L0_gnn_in['upd_b2'], 'L0_gnn_att_W1': _L0_gnn_in['att_W1'], 'L0_gnn_att_b1': _L0_gnn_in['att_b1'], 'L0_gnn_att_W2': _L0_gnn_in['att_W2'], 'L0_gnn_att_b2': _L0_gnn_in['att_b2'], 'L0_gnn_glb_W': _L0_gnn_in['glb_W'], 'L0_gnn_glb_b': _L0_gnn_in['glb_b'], 'L1_gnn_Wq': _L1_gnn_in['Wq'], 'L1_gnn_bq': _L1_gnn_in['bq'], 'L1_gnn_Wk': _L1_gnn_in['Wk'], 'L1_gnn_bk': _L1_gnn_in['bk'], 'L1_gnn_Wv': _L1_gnn_in['Wv'], 'L1_gnn_bv': _L1_gnn_in['bv'], 'L1_gnn_Wl': _L1_gnn_in['Wl'], 'L1_gnn_bl': _L1_gnn_in['bl']}

def reference(x, src, dst, L0_gnn_msg_W1, L0_gnn_msg_b1, L0_gnn_msg_W2, L0_gnn_msg_b2, L0_gnn_upd_W1, L0_gnn_upd_b1, L0_gnn_upd_W2, L0_gnn_upd_b2, L0_gnn_att_W1, L0_gnn_att_b1, L0_gnn_att_W2, L0_gnn_att_b2, L0_gnn_glb_W, L0_gnn_glb_b, L1_gnn_Wq, L1_gnn_bq, L1_gnn_Wk, L1_gnn_bk, L1_gnn_Wv, L1_gnn_bv, L1_gnn_Wl, L1_gnn_bl):
    import jax
    import jax.numpy as jnp

    def _L0_gnn_ref(x, edge_index, msg_W1, msg_b1, msg_W2, msg_b2, upd_W1, upd_b1, upd_W2, upd_b2, att_W1, att_b1, att_W2, att_b2, glb_W, glb_b):
        import jax, jax.numpy as jnp
        import numpy as np
        D = 128
        STEPS = 2
        N = 50000
        E = 15625

        def _mlp2(h, W1, b1, W2, b2):
            return jax.nn.relu(h @ W1 + b1) @ W2 + b2
        num_nodes = x.shape[0]
        src, dst = (edge_index[0], edge_index[1])
        global_repr = jax.nn.relu(jnp.mean(x, axis=0, keepdims=True) @ glb_W + glb_b)
        h = x
        for _ in range(STEPS):
            edge_feat = jnp.concatenate([h[src], h[dst]], axis=-1)
            messages = _mlp2(edge_feat, msg_W1, msg_b1, msg_W2, msg_b2)
            att = jax.nn.sigmoid(_mlp2(edge_feat, att_W1, att_b1, att_W2, att_b2))
            weighted = messages * att
            aggregated = jax.ops.segment_sum(weighted, dst, num_segments=num_nodes)
            combined = jnp.concatenate([h, aggregated], axis=-1)
            new_h = _mlp2(combined, upd_W1, upd_b1, upd_W2, upd_b2)
            h = new_h + h + global_repr
        return h

    def _L1_gnn_ref(feature, Wq, bq, Wk, bk, Wv, bv, Wl, bl, src, dst):
        import jax, jax.numpy as jnp
        import numpy as np
        N_NODES = 50000
        N_EDGES = 25000
        D_IN = 128
        D_OUT = 128
        n = feature.shape[0]
        q = feature @ Wq + bq
        k = feature @ Wk + bk
        v = feature @ Wv + bv
        s = jnp.sum(q[dst] * k[src], axis=-1)
        m = jax.ops.segment_max(s, dst, num_segments=n)
        e = jnp.exp(s - m[dst])
        denom = jax.ops.segment_sum(e, dst, num_segments=n)
        w = e / denom[dst]
        agg = jax.ops.segment_sum(w[:, None] * v[src], dst, num_segments=n)
        deg = jax.ops.segment_sum(jnp.ones_like(s), dst, num_segments=n)
        v_out = jnp.where(deg[:, None] > 0, agg, v)
        return jax.nn.relu(v_out @ Wl + bl)
    edge_index = jnp.stack([src, dst])
    x = _layernorm(x + _L0_gnn_ref(x, edge_index, L0_gnn_msg_W1, L0_gnn_msg_b1, L0_gnn_msg_W2, L0_gnn_msg_b2, L0_gnn_upd_W1, L0_gnn_upd_b1, L0_gnn_upd_W2, L0_gnn_upd_b2, L0_gnn_att_W1, L0_gnn_att_b1, L0_gnn_att_W2, L0_gnn_att_b2, L0_gnn_glb_W, L0_gnn_glb_b), axis=-1)
    x = _layernorm(x + _L1_gnn_ref(x, L1_gnn_Wq, L1_gnn_bq, L1_gnn_Wk, L1_gnn_bk, L1_gnn_Wv, L1_gnn_bv, L1_gnn_Wl, L1_gnn_bl, src, dst), axis=-1)
    return x

_drawn_inputs = setup_inputs


def setup_inputs(seed=0):
    import zlib

    import numpy as np

    out = dict(_drawn_inputs(seed))
    spreads = {'L0_gnn_msg_b1': (0.0, 0.1),
     'L0_gnn_msg_b2': (0.0, 0.1),
     'L0_gnn_upd_b1': (0.0, 0.1),
     'L0_gnn_upd_b2': (0.0, 0.1),
     'L0_gnn_att_b1': (0.0, 0.8),
     'L0_gnn_glb_b': (0.0, 0.1)}
    factors = {'L0_gnn_glb_W': 8.0, 'L1_gnn_bq': 3.07, 'L1_gnn_bk': 8.0}
    for name, (base, spread) in spreads.items():
        noise = np.random.default_rng([zlib.crc32(name.encode()), seed]).standard_normal(out[name].shape)
        drawn = base * np.exp(spread * noise) if base else spread * noise
        out[name] = jnp.asarray(drawn.astype(out[name].dtype))
    for name, factor in factors.items():
        out[name] = (out[name] * factor).astype(out[name].dtype)
    return out
```

```python
import concourse.bass as bass
import concourse.mybir as mybir
import numpy as np
from contextlib import ExitStack

F32, BF16, I32 = mybir.dt.float32, mybir.dt.bfloat16, mybir.dt.int32
ALU, ACT, AX = mybir.AluOpType, mybir.ActivationFunctionType, mybir.AxisListType

P = 128
N, E, D = 3125, 100000, 128
NT = 26
NPAD = NT * P
CH = NPAD // 8
TG = 8
NG = 98
BODIES = NG // 2
WIN = 42
PAIRS = TG // 2
LAYERS = 2
ROUNDS = -(-(N + 1) // WIN)
BIG = 3.0e38
PIECE = CH // 4
EPS = 1e-5


def build(nc, x, idx, dst_pm, dst_gm, w, out):
    A_tab = nc.dram_tensor("A_tab", (NPAD, 2 * D), F32, kind="Internal").ap()
    B_tab = nc.dram_tensor("B_tab", (NPAD, 3 * 2 * D), BF16, kind="Internal").ap()
    X_tab = nc.dram_tensor("X_tab", (NPAD, D), F32, kind="Internal").ap()
    Q_tab = nc.dram_tensor("Q_tab", (NPAD, 3 * (D + 1)), BF16, kind="Internal").ap()

    with ExitStack() as ctx:
        def sb(name, shape, dt=F32):
            return ctx.enter_context(nc.sbuf_tensor(name, shape, dt))

        def pb(name, shape, dt=F32):
            return ctx.enter_context(nc.psum_tensor(name, shape, dt))

        def sem(name):
            return ctx.enter_context(nc.semaphore(name))

        def sems(name, *dims):
            if not dims:
                return sem(name)
            return [sems(f"{name}_{k}", *dims[1:]) for k in range(dims[0])]

        hT = sb("hT", [P, NPAD])
        xT = sb("xT", [P, NPAD])
        xN = sb("xN", [P, NT, D])
        acc = sb("acc", [P, 2, NPAD])
        mrun = sb("mrun", [P, NPAD])
        ident = sb("ident", [P, P])
        ones = sb("ones", [P, P])
        inv_d = sb("inv_d", [P, P])
        iota_w = sb("iota_w", [P, 3, WIN])
        eps_c = sb("eps_c", [P, 1])
        dstI = sb("dstI", [P, NG * TG], I32)
        dst0 = sb("dst0", [P, NG * TG])
        dst_rel = sb("dst_rel", [P, NG * TG])
        rowsI = sb("rowsI", [NG, TG * P], I32)
        rmin = sb("rmin", [NG, 1])
        rmax = sb("rmax", [NG, 1])
        span = sb("span", [NG, 1])
        base0 = sb("base0", [1, NG])
        baseF = sb("baseF", [1, NG])
        baseI = sb("baseI", [1, NG], I32)
        spanm = sb("spanm", [1, 1])
        steps = sb("steps", [1, ROUNDS])
        within = sb("within", [1, ROUNDS])
        count = sb("count", [1, 1])
        roundsI = sb("roundsI", [1, 1], I32)
        wcat = sb("wcat", [P, 4 * D])
        b1row = sb("b1row", [1, 2 * D])
        attw = sb("attw", [P, D])
        attb = sb("attb", [P, 1])
        msgW2 = sb("msgW2", [P, D])
        b2row = sb("b2row", [1, D])
        updW1 = sb("updW1", [P, 2, D])
        updW2 = sb("updW2", [P, D])
        glbW = sb("glbW", [P, D])
        Wq = sb("Wq", [P, D])
        Wk = sb("Wk", [P, D])
        WkTb = sb("WkTb", [P, D + 1])
        Wv = sb("Wv", [P, D])
        Wl = sb("Wl", [P, D])
        cols = sb("cols", [P, 8])
        UB1, UB2, GLB, BQ, BV, BL, SUMX, GH = range(8)
        gcol = sb("gcol", [P, 1])

        def col(k):
            return cols[:, k:k + 1]

        idx_st = sb("idx_st", [P, 2, TG], I32)
        arow = sb("arow", [P, 2, TG, 2 * D])
        xrow = sb("xrow", [P, 2, TG, D + 1])
        bwin = sb("bwin", [3 * WIN, 2, 2 * D], BF16)
        qwin = sb("qwin", [3 * WIN, 2, D + 1], BF16)
        oh = sb("oh", [P, 2, TG, 3 * WIN])
        oht = sb("oht", [3 * WIN, 2, TG * P], BF16)
        mask = sb("mask", [WIN, 2, TG * P], BF16)
        pre = sb("pre", [P, 2, TG, 2 * D])
        zw = sb("zw", [P, 2, TG, D + 1])
        junk = sb("junk", [P, TG, D + 1], BF16)
        junkm = sb("junkm", [WIN, TG * P], BF16)
        lg = sb("lg", [P, 2, TG])
        wt = sb("wt", [P, 2, TG])
        sm = sb("sm", [P, TG])
        ssum = sb("ssum", [WIN, 2, D + 1])
        me = sb("me", [P, TG])
        mloc = sb("mloc", [WIN, 1])
        mres = sb("mres", [WIN, 1])
        m3 = sb("m3", [WIN, 3], BF16)
        mnew = sb("mnew", [P, WIN])
        diff = sb("diff", [P, 2, WIN])
        ed = sb("ed", [P, 2, WIN])
        newsc = sb("newsc", [P, 2, WIN])
        oldsc = sb("oldsc", [P, 2, WIN])
        stage = sb("stage", [P, 2, 2, P])
        tabA = sb("tabA", [P, 2, 2 * D])
        tabB = sb("tabB", [P, 2, 3, 2 * D], BF16)
        res = sb("res", [P, 2, 2 * D])
        aggs = sb("aggs", [P, 2, CH])
        hid = sb("hid", [P, 2, CH])
        t1 = sb("t1", [P, 2, CH])
        t2 = sb("t2", [P, 2, CH])
        t3 = sb("t3", [P, 2, CH])
        outn = sb("outn", [PIECE, 2, 4, D])


        psum = pb("psum_main", [P, 6 * 512])
        bank = [psum[:, k * 512:(k + 1) * 512] for k in range(6)]
        scat = [pb(f"scat{k}", [P, 512]) for k in range(2)]
        bg = [bank[k].rearrange("p (t n) -> p t n", t=2) for k in range(4)]
        ohp = [bank[4], bank[5]]
        score_ps = psum[0:WIN, 2 * 512:4 * 512]
        sc_sum = [scat[k][:, 256:256 + 2 * WIN].rearrange("p (a n) -> p a n", a=2) for k in range(2)]
        sc_max = bank[2][:, 0:WIN]
        sc_me = bank[2][:, WIN:WIN + 3 * TG].rearrange("p (t k) -> p t k", k=3)

        loaded, loaded_tail = sem("loaded"), sem("loaded_tail")
        const_done = sem("const_done")
        ident_done = sem("ident_done")
        setup_dve, setup_pe, setup_act = sem("setup_dve"), sem("setup_pe"), sem("setup_act")
        xt_ps, xt_done = sem("xt_ps"), sem("xt_done")
        ready_all = sem("ready_all")
        moved = sem("moved")
        base_ready = sem("base_ready")
        acc_zero = sem("acc_zero")
        staged, tab_ps, a_copied, hi_done, res_done, mid_done, lo_done, a_out, b_out = (sems(n, 2) for n in (
            "staged", "tab_ps", "a_copied", "hi_done", "res_done", "mid_done", "lo_done", "a_out", "b_out"))
        idx_ld, win_ld = sems("idx_ld", 2), sems("win_ld", 2)
        gathered = sems("gathered", 2, PAIRS)
        oh_ready, ohp_ready, oht_ready = sems("oh_ready", 2), sems("ohp_ready", 2, 2), sems("oht_ready", 2, 2)
        picked, dotted = sems("picked", 2, PAIRS), sems("dotted", 2, PAIRS)
        added, att_done = sems("added", 2, PAIRS), sems("att_done", 2, PAIRS)
        zw_ready, summed, sum_out, scat_done, merged = (sems(n, 2) for n in (
            "zw_ready", "summed", "sum_out", "scat_done", "merged"))
        u_agg, u_aggc, u_hid, u_relu, u_new, u_h = (sems(n, 2) for n in (
            "u_agg", "u_aggc", "u_hid", "u_relu", "u_new", "u_h"))
        n_y, n_mu, n_d, n_sq, n_var, n_std, n_r, n_x1, n_lin, n_linc = (sems(n, 2) for n in (
            "n_y", "n_mu", "n_d", "n_sq", "n_var", "n_std", "n_r", "n_x1", "n_lin", "n_linc"))
        (s_spread, s_max, s_hi, s_mid, s_lo, s_me, s_mer, s_sub, s_w, s_mnew, s_diff, s_ed, s_scaled) = (
            sem(n) for n in ("s_spread", "s_max", "s_hi", "s_mid", "s_lo", "s_me", "s_mer", "s_sub", "s_w",
                             "s_mnew", "s_diff", "s_ed", "s_scaled"))
        f_inv, f_avg, f_sel, f_l, f_o, f_t, f_n = (sems(n, 2) for n in (
            "f_inv", "f_avg", "f_sel", "f_l", "f_o", "f_t", "f_n"))
        out_sem = sems("out_sem", 2)

        block = ctx.enter_context(nc.Block())
        LOADS = 27
        FULL, REST = N // P, N % P
        TB = NT // 2
        CB = NPAD // CH // 2
        GROUPS4 = list(range(0, NT, 4))

        def rounds(eng):
            eng.wait_ge(ready_all, 1)
            eng.nop(nofuse=True)
            return eng.value_load(roundsI[0:1, 0:1], min_val=1, max_val=ROUNDS)

        def window(eng, g):
            return eng.value_load(baseI[0:1, bass.ds(g, 1)], min_val=0, max_val=NPAD - WIN)

        def chunk(t, c):
            return t[:, bass.ds(c * CH, CH)]

        def group_tick(r, g):
            return r * NG + g + 1

        def pipeline(eng, p, step, tail):
            t0 = p * BODIES
            step(0, 0, t0 + 1, t0, t0 + 1, False, True)
            with eng.Fori(0, BODIES - 1) as j:
                step(2 * j + 1, 1, t0 + j + 1, t0 + j + 1, t0 + j + 2, True, True)
                step(2 * j + 2, 0, t0 + j + 2, t0 + j + 1, t0 + j + 2, True, True)
            step(NG - 1, 1, t0 + BODIES, t0 + BODIES, t0 + BODIES + 1, True, False)
            tail(NG - 1, 1, t0 + BODIES)

        @block.sync
        def _(sp):
            def load(dst, src):
                sp.dma_start(dst, src).then_inc(loaded, 16)

            load(xN[:, 0:FULL, :], x[0:FULL * P, :].rearrange("(t p) d -> p t d", p=P))
            load(rowsI[:, :], dst_gm)
            load(dstI[:, :], dst_pm)
            for k, (name, half) in enumerate((("msg_W1", 0), ("att_W1", 0), ("msg_W1", 1), ("att_W1", 1))):
                load(wcat[:, k * D:(k + 1) * D], w[name][half * D:(half + 1) * D, :])
            load(b1row[0:1, 0:D], w["msg_b1"].rearrange("(a d) -> a d", a=1))
            load(b1row[0:1, D:2 * D], w["att_b1"].rearrange("(a d) -> a d", a=1))
            for dst, name in ((msgW2, "msg_W2"), (updW2, "upd_W2"), (glbW, "glb_W"), (Wq, "Wq"), (Wk, "Wk"),
                              (Wv, "Wv"), (Wl, "Wl")):
                load(dst[:, :], w[name])
            load(updW1[:, :, :], w["upd_W1"].rearrange("(a k) n -> k a n", a=2))
            load(attw[:, :], w["att_W2"].rearrange("d a -> a d").broadcast_to([P, D]))
            load(attb[:, :], w["att_b2"].rearrange("(a d) -> a d", a=1).broadcast_to([P, 1]))
            load(b2row[0:1, :], w["msg_b2"].rearrange("(a d) -> a d", a=1))
            load(WkTb[:, D:D + 1], w["bk"].rearrange("(p a) -> p a", a=1))
            for k, name in ((UB1, "upd_b1"), (UB2, "upd_b2"), (GLB, "glb_b"), (BQ, "bq"), (BV, "bv"), (BL, "bl")):
                load(col(k), w[name].rearrange("(p a) -> p a", a=1))
            sp.wait_ge(const_done, 1)
            sp.nop(nofuse=True)
            sp.dma_start(xN[0:REST, FULL, :], x[FULL * P:N, :]).then_inc(loaded_tail, 16)
            for s in (a_out, b_out):
                for u in range(2):
                    sp.sem_inc(s[u], 16)
            for u in range(2):
                sp.sem_inc(out_sem[u], 64)
            R = rounds(sp)

            def one_pass(p, win, tab):
                sp.wait_ge(base_ready, p + 1)
                sp.nop(nofuse=True)

                width = win.shape[2]

                def step(g, u, ticks):
                    if ticks is not None:
                        for q in range(PAIRS):
                            sp.wait_ge(gathered[u][q], ticks * 32)
                            sp.nop(nofuse=True)
                    sp.dma_start(idx_st[:, u, :], idx[bass.ds(g * P, P), :]).then_inc(idx_ld[u], 16)
                    row = window(sp, g)
                    if ticks is not None:
                        sp.wait_ge(picked[u][PAIRS - 1], ticks)
                        sp.nop(nofuse=True)
                    for k in range(3):
                        sp.dma_start(win[k * WIN:(k + 1) * WIN, u, :],
                                     tab[bass.ds(row, WIN), k * width:(k + 1) * width]).then_inc(win_ld[u], 16)

                step(0, 0, None)
                step(1, 1, None)
                with sp.Fori(1, BODIES) as j:
                    step(2 * j, 0, p * BODIES + j)
                    step(2 * j + 1, 1, p * BODIES + j)

            def store_tables(q, rows, row_n, parts, parts_n):
                with sp.Fori(0, TB) as b:
                    for u in range(2):
                        n = q * TB + b + 1
                        at = bass.ds((2 * b + u) * P, P)
                        sp.wait_ge(a_copied[u], n)
                        sp.nop(nofuse=True)
                        sp.dma_start(rows[at, :], tabA[:, u, 0:row_n]).then_inc(a_out[u], 16)
                        sp.wait_ge(lo_done[u], n)
                        sp.nop(nofuse=True)
                        sp.dma_start(parts[at, :].rearrange("p (k d) -> p k d", k=3),
                                     tabB[:, u, :, 0:parts_n]).then_inc(b_out[u], 16)
                for u in range(2):
                    sp.wait_ge(b_out[u], (q + 1) * (TB * 16) + 16)
                    sp.nop(nofuse=True)

            with sp.Fori(0, LAYERS) as l:
                store_tables(l, A_tab, 2 * D, B_tab, 2 * D)
                with sp.Fori(0, R) as r:
                    one_pass(l * R + r, bwin, B_tab)
            store_tables(LAYERS, X_tab, D, Q_tab, D + 1)
            with sp.Fori(0, R) as r:
                one_pass(LAYERS * R + r, qwin, Q_tab)

            def store_out(c, u, n, known):
                sp.wait_ge(f_n[u], n)
                sp.nop(nofuse=True)
                for k in range(4):
                    m = PIECE if known is None else min(PIECE, N - known * CH - k * PIECE)
                    if m > 0:
                        at = c * CH + k * PIECE
                        rows = bass.ds(at, PIECE) if known is None else slice(at, at + m)
                        sp.dma_start(out[rows, :], outn[0:m, u, k, :]).then_inc(out_sem[u], 16)

            with sp.Fori(0, CB - 1) as b:
                store_out(2 * b, 0, b + 1, None)
                store_out(2 * b + 1, 1, b + 1, None)
            last = 2 * (CB - 1)
            store_out(last, 0, CB, last)
            store_out(last + 1, 1, CB, last + 1)
            for u in range(2):
                pieces = sum(min(4, max(0, -(-(N - c * CH) // PIECE))) for c in range(u, 2 * CB, 2))
                sp.wait_ge(out_sem[u], 64 + 16 * pieces)
                sp.nop(nofuse=True)

        @block.gpsimd
        def _(pool):
            nc.gpsimd.memset(ident[:, :], 0.0).then_inc(ident_done, 1)
            nc.gpsimd.iota(iota_w[:, :, :], pattern=[[0, 3], [1, WIN]], base=0, channel_multiplier=0,
                           allow_small_or_imprecise_dtypes=True).then_inc(ident_done, 1)
            nc.gpsimd.iota(steps[:, :], pattern=[[WIN, ROUNDS]], base=0, channel_multiplier=0,
                           allow_small_or_imprecise_dtypes=True).then_inc(ident_done, 1)
            pool.wait_ge(ident_done, 3)
            pool.nop(nofuse=True)
            nc.gpsimd.affine_select(out=ident[:, :], in_=ident[:, :], compare_op=ALU.not_equal, fill=1.0,
                                    base=0, pattern=[[-1, P]], channel_multiplier=1).then_inc(ident_done, 1)
            R = rounds(pool)

            def middle_parts(q, width):
                with pool.Fori(0, TB) as b:
                    for u in range(2):
                        pool.wait_ge(res_done[u], q * TB + b + 2)
                        pool.nop(nofuse=True)
                        nc.gpsimd.tensor_copy(tabB[:, u, 1, 0:width], res[:, u, 0:width]).then_inc(mid_done[u], 1)
                for u in range(2):
                    pool.wait_ge(a_out[u], (q + 1) * (TB * 16) + 16)
                    pool.nop(nofuse=True)

            def gather(p, freed, rows, tab):
                with pool.Fori(0, BODIES) as j:
                    n = p * BODIES + j + 1
                    for u in range(2):
                        pool.wait_ge(idx_ld[u], n * 16)
                        pool.nop(nofuse=True)
                        for t in range(TG):
                            freed(u, t, n)
                            nc.gpsimd.indirect_dma_start(
                                rows(u, t), None, tab,
                                bass.IndirectOffsetOnAxis(ap=idx_st[:, u, t:t + 1], axis=0)).then_inc(gathered[u][t // 2], 16)

            def added_to(u, t, n):
                if t % 2 == 0:
                    pool.wait_ge(added[u][t // 2], n)
                    pool.nop(nofuse=True)

            def weighted(u, t, n):
                if t == 0:
                    pool.wait_ge(zw_ready[u], n - 1)
                    pool.nop(nofuse=True)

            with pool.Fori(0, LAYERS) as l:
                pool.wait_ge(u_h[1], l * CB + 1)
                pool.nop(nofuse=True)
                nc.gpsimd.memset(acc[:, :, :], 0.0).then_inc(acc_zero, 1)
                middle_parts(l, 2 * D)
                with pool.Fori(0, R) as r:
                    gather(l * R + r, added_to, lambda u, t: arow[:, u, t, :], A_tab)
            pool.wait_ge(u_h[1], LAYERS * CB + 1)
            pool.nop(nofuse=True)
            nc.gpsimd.memset(acc[:, :, :], 0.0).then_inc(acc_zero, 1)
            nc.gpsimd.memset(mrun[:, :], -BIG / 2).then_inc(acc_zero, 1)
            middle_parts(LAYERS, D + 1)
            with pool.Fori(0, R) as r:
                gather(LAYERS * R + r, weighted, lambda u, t: xrow[:, u, t, 0:D], X_tab)

        @block.scalar
        def _(act):
            for k, first in enumerate(GROUPS4):
                m = min(4, NT - first)
                act.wait_ge(xt_ps, k + 1)
                act.nop(nofuse=True)
                nc.scalar.copy(xT[:, first * P:(first + m) * P], bank[k % 2][:, 0:m * P]).then_inc(xt_done, 1)
            act.wait_ge(setup_pe, 3)
            act.nop(nofuse=True)
            nc.scalar.activation(col(GH), bank[3][:, 0:1], ACT.Relu, bias=col(GLB)).then_inc(setup_act, 1)
            R = rounds(act)

            def tables(q, width, b_at, a_width, with_q):
                with act.Fori(0, TB) as b:
                    n = q * TB + b + 1
                    for u in range(2):
                        at = bass.ds((2 * b + u) * P, P)
                        if with_q:
                            nc.scalar.copy(stage[:, u, 1, :], xT[:, at])
                        nc.scalar.copy(stage[:, u, 0, :], hT[:, at]).then_inc(staged[u], 1)
                    for u in range(2):
                        act.wait_ge(tab_ps[u], n)
                        act.nop(nofuse=True)
                        act.wait_ge(a_out[u], n * 16)
                        act.nop(nofuse=True)
                        nc.scalar.copy(tabA[:, u, 0:a_width], bank[u][:, 0:a_width]).then_inc(a_copied[u], 1)
                        act.wait_ge(b_out[u], n * 16)
                        act.nop(nofuse=True)
                        nc.scalar.copy(tabB[:, u, 0, 0:width], bank[u][:, b_at:b_at + width]).then_inc(hi_done[u], 1)

            def transposed(u, n, masked):
                for h in range(2):
                    act.wait_ge(ohp_ready[u][h], n)
                    act.nop(nofuse=True)
                    part = slice(h * 512, (h + 1) * 512)
                    if masked:
                        nc.scalar.activation(mask[:, u, part], ohp[h][0:WIN, :], ACT.Copy, scale=BIG / 2, bias=-BIG / 2)
                    nc.scalar.copy(oht[:, u, part], ohp[h][0:3 * WIN, :]).then_inc(oht_ready[u][h], 1)

            def sums_out(u, n):
                act.wait_ge(summed[u], n)
                act.nop(nofuse=True)
                nc.scalar.copy(ssum[:, u, :], scat[u][0:WIN, 0:D + 1]).then_inc(sum_out[u], 1)

            def message_pass(p):
                def step(g, u, n, m, k, prev, nxt):
                    for q in range(PAIRS):
                        if q == PAIRS - 1 and nxt:
                            transposed(1 - u, k, False)
                        two = slice(2 * q, 2 * q + 2)
                        act.wait_ge(dotted[u][q], n)
                        act.nop(nofuse=True)
                        nc.scalar.activation(zw[:, u, two, D], lg[:, u, two], ACT.Sigmoid,
                                             bias=attb[:, :]).then_inc(att_done[u][q], 1)
                        act.wait_ge(att_done[u][q], n)
                        act.nop(nofuse=True)
                        for t in (2 * q, 2 * q + 1):
                            ins = nc.scalar.activation(zw[:, u, t, 0:D], pre[:, u, t, 0:D], ACT.Relu,
                                                       scale=zw[:, u, t, D:D + 1])
                        if q == 1 and prev:
                            sums_out(1 - u, m)
                    ins.then_inc(zw_ready[u], 1)

                transposed(0, p * BODIES + 1, False)
                pipeline(act, p, step, lambda g, u, n: sums_out(u, n))

            def update(l):
                with act.Fori(0, CB) as b:
                    n = l * CB + b + 1
                    for u in range(2):
                        act.wait_ge(u_agg[u], n)
                        act.nop(nofuse=True)
                        nc.scalar.copy(aggs[:, u, :], bank[u][:, 0:CH]).then_inc(u_aggc[u], 1)
                    for u in range(2):
                        act.wait_ge(u_hid[u], n)
                        act.nop(nofuse=True)
                        nc.scalar.activation(hid[:, u, :], bank[2 + u][:, 0:CH], ACT.Relu,
                                             bias=col(UB1)).then_inc(u_relu[u], 1)

            with act.Fori(0, LAYERS) as l:
                act.wait_ge(u_h[1], l * CB + 1)
                act.nop(nofuse=True)
                tables(l, 2 * D, 2 * D, 2 * D, False)
                with act.Fori(0, R) as r:
                    message_pass(l * R + r)
                update(l)

            def norm(q):
                for u in range(2):
                    act.wait_ge(n_d[u], q)
                    act.nop(nofuse=True)
                    nc.scalar.activation(t3[:, u, :], t2[:, u, :], ACT.Square).then_inc(n_sq[u], 1)
                for u in range(2):
                    act.wait_ge(n_var[u], q)
                    act.nop(nofuse=True)
                    nc.scalar.activation(t3[:, u, :], bank[2 + u][:, 0:CH], ACT.Sqrt,
                                         bias=eps_c[:, :]).then_inc(n_std[u], 1)

            with act.Fori(0, CB) as b:
                norm(b + 1)
                for u in range(2):
                    act.wait_ge(n_lin[u], b + 1)
                    act.nop(nofuse=True)
                    nc.scalar.activation(chunk(xT, 2 * b + u), bank[4 + u][:, 0:CH], ACT.Identity,
                                         bias=col(BQ)).then_inc(n_linc[u], 1)
            act.wait_ge(n_x1[1], CB)
            act.nop(nofuse=True)
            for u in range(2):
                act.wait_ge(n_linc[u], CB)
                act.nop(nofuse=True)
            tables(LAYERS, D + 1, D, D, True)

            def attention_pass(p, r):
                def step(g, u, n, m, k, prev, nxt):
                    a = group_tick(r, g)
                    if prev:
                        sums_out(1 - u, m)
                    if nxt:
                        transposed(1 - u, k, True)
                    act.wait_ge(s_sub, a)
                    act.nop(nofuse=True)
                    nc.scalar.activation(wt[:, u, :], sm[:, :], ACT.Exp).then_inc(s_w, 1)
                    act.wait_ge(s_w, a)
                    act.nop(nofuse=True)
                    for t in range(TG):
                        ins = nc.scalar.activation(zw[:, u, t, :], xrow[:, u, t, :], ACT.Copy,
                                                   scale=wt[:, u, t:t + 1])
                    ins.then_inc(zw_ready[u], 1)
                    act.wait_ge(s_diff, a)
                    act.nop(nofuse=True)
                    nc.scalar.activation(ed[:, :, :], diff[:, :, :], ACT.Exp).then_inc(s_ed, 1)

                transposed(0, p * BODIES + 1, True)
                pipeline(act, p, step, lambda g, u, n: sums_out(u, n))

            with act.Fori(0, R) as r:
                attention_pass(LAYERS * R + r, r)

            with act.Fori(0, CB) as b:
                n = b + 1
                for u in range(2):
                    act.wait_ge(n_lin[u], CB + n)
                    act.nop(nofuse=True)
                    nc.scalar.activation(t2[:, u, :], bank[u][:, 0:CH], ACT.Identity, bias=col(BV)).then_inc(n_linc[u], 1)
                for u in range(2):
                    act.wait_ge(f_l[u], n)
                    act.nop(nofuse=True)
                    nc.scalar.activation(t3[:, u, :], bank[2 + u][:, 0:CH], ACT.Relu, bias=col(BL)).then_inc(f_o[u], 1)
                norm(CB + n)
                for u in range(2):
                    act.wait_ge(f_t[u], n)
                    act.nop(nofuse=True)
                    act.wait_ge(out_sem[u], n * 64)
                    act.nop(nofuse=True)
                    nc.scalar.copy(outn[:, u, :, :], bank[4 + u][0:PIECE, :].rearrange("p (k d) -> p k d", k=4)
                                   ).then_inc(f_n[u], 1)

        @block.vector
        def _(v):
            v_ = nc.vector
            v_.memset(xN[:, FULL:NT, :], 0.0).then_inc(const_done, 1)
            v_.memset(ones[:, :], 1.0)
            v_.memset(inv_d[:, :], 1.0 / D)
            v_.memset(eps_c[:, :], EPS)
            v_.memset(xrow[:, :, :, D:D + 1], 1.0).then_inc(const_done, 1)
            for s in (added[0] + added[1], res_done):
                for one in s:
                    v.sem_inc(one, 1)
            v.wait_ge(loaded, 16 * LOADS)
            v.nop(nofuse=True)
            v_.tensor_reduce(rmin[:, :], rowsI[:, :], AX.X, ALU.min).then_inc(setup_dve, 1)
            v_.tensor_reduce(rmax[:, :], rowsI[:, :], AX.X, ALU.max).then_inc(setup_dve, 1)
            v.wait_ge(setup_dve, 2)
            v.nop(nofuse=True)
            v_.tensor_tensor(span[:, :], rmax[:, :], rmin[:, :], ALU.subtract).then_inc(setup_dve, 1)
            v.wait_ge(setup_pe, 1)
            v.nop(nofuse=True)
            v_.tensor_copy(base0[:, :], bank[2][0:1, 0:NG])
            v_.tensor_reduce(spanm[:, :], bank[2][0:1, NG:2 * NG], AX.X, ALU.max).then_inc(setup_dve, 1)
            v_.tensor_tensor(dst0[:, :].rearrange("p (g t) -> p g t", t=TG),
                             dstI[:, :].rearrange("p (g t) -> p g t", t=TG),
                             bank[2][:, 2 * NG:3 * NG].unsqueeze(2).to_broadcast([P, NG, TG]), ALU.subtract)
            v.wait_ge(setup_dve, 4)
            v.nop(nofuse=True)
            v.wait_ge(ident_done, 4)
            v.nop(nofuse=True)
            v_.tensor_scalar(within[:, :], steps[:, :], spanm[:, :], None, ALU.is_le).then_inc(setup_dve, 1)
            v.wait_ge(setup_dve, 5)
            v.nop(nofuse=True)
            v_.reduce_sum(count[:, :], within[:, :], AX.X).then_inc(setup_dve, 1)
            v.wait_ge(setup_dve, 6)
            v.nop(nofuse=True)
            v_.tensor_copy(roundsI[:, :], count[:, :]).then_inc(ready_all, 1)
            for k, first in enumerate(GROUPS4):
                m = min(4, NT - first)
                v.wait_ge(xt_done, k + 1)
                v.nop(nofuse=True)
                v_.tensor_copy(hT[:, first * P:(first + m) * P], xT[:, first * P:(first + m) * P])
            v_.reduce_sum(col(SUMX), xT[:, 0:N], AX.X).then_inc(setup_dve, 1)
            v.wait_ge(setup_dve, 7)
            v.nop(nofuse=True)
            v_.tensor_scalar(col(SUMX), col(SUMX), 1.0 / N, None, ALU.mult).then_inc(setup_dve, 1)
            v.wait_ge(setup_act, 1)
            v.nop(nofuse=True)
            v_.tensor_copy(WkTb[:, 0:D], bank[3][:, P:2 * P]).then_inc(u_h[0], 1)
            v_.tensor_tensor(gcol[:, :], col(GH), col(UB2), ALU.add).then_inc(u_h[1], 1)
            R = rounds(v)

            def split(q, width, b_at):
                with v.Fori(0, TB) as b:
                    n = q * TB + b + 1
                    for u in range(2):
                        v.wait_ge(hi_done[u], n)
                        v.nop(nofuse=True)
                        v_.tensor_tensor(res[:, u, 0:width], bank[u][:, b_at:b_at + width], tabB[:, u, 0, 0:width],
                                         ALU.subtract).then_inc(res_done[u], 1)
                    for u in range(2):
                        v.wait_ge(mid_done[u], n)
                        v.nop(nofuse=True)
                        v_.tensor_tensor(tabB[:, u, 2, 0:width], res[:, u, 0:width], tabB[:, u, 1, 0:width],
                                         ALU.subtract).then_inc(lo_done[u], 1)

            def write_base():
                v_.tensor_scalar(baseI[:, :], baseF[:, :], float(NPAD - WIN), None, ALU.min).then_inc(base_ready, 1)

            def all_rounds(l, one_pass):
                t0 = l * (R + 1)
                v_.tensor_copy(baseF[:, :], base0[:, :])
                v_.tensor_copy(dst_rel[:, :], dst0[:, :]).then_inc(moved, 1)
                v.wait_ge(moved, t0 + 1)
                v.nop(nofuse=True)
                with v.Fori(0, R) as r:
                    write_base()
                    one_pass(r)
                    v_.tensor_scalar(baseF[:, :], baseF[:, :], float(WIN), None, ALU.add)
                    v_.tensor_scalar(dst_rel[:, :], dst_rel[:, :], float(-WIN), None, ALU.add).then_inc(moved, 1)
                    v.wait_ge(moved, t0 + r + 2)
                    v.nop(nofuse=True)

            def one_hot(g, u):
                rel = dst_rel[:, bass.ds(g * TG, TG)].unsqueeze(2).to_broadcast([P, TG, 3 * WIN])
                nodes = iota_w[:, :, :].rearrange("p k n -> p (k n)").unsqueeze(1).to_broadcast([P, TG, 3 * WIN])
                v_.tensor_tensor(oh[:, u, :, :], nodes, rel,
                                 ALU.is_equal).then_inc(oh_ready[u], 1)

            def message_pass(p):
                def add(u, n, q):
                    v.wait_ge(picked[u][q], n)
                    v.nop(nofuse=True)
                    v.wait_ge(gathered[u][q], n * 32)
                    v.nop(nofuse=True)
                    v_.tensor_tensor(pre[:, u, 2 * q:2 * q + 2, :], arow[:, u, 2 * q:2 * q + 2, :], bg[q],
                                     ALU.add).then_inc(added[u][q], 1)

                def dot(u, n, q):
                    v.wait_ge(added[u][q], n + 1)
                    v.nop(nofuse=True)
                    for t in (2 * q, 2 * q + 1):
                        ins = v_.scalar_tensor_tensor(out=junk[:, t, 0:D], in0=pre[:, u, t, D:2 * D], scalar=0.0,
                                                      in1=attw[:, :], op0=ALU.max, op1=ALU.mult,
                                                      accum_out=lg[:, u, t:t + 1])
                    ins.then_inc(dotted[u][q], 1)

                def merge(g, u, n):
                    row = window(v, g)
                    v.wait_ge(scat_done[u], n)
                    v.nop(nofuse=True)
                    at = acc[:, :, bass.ds(row, WIN)]
                    v_.tensor_tensor(at, at, sc_sum[u], ALU.add).then_inc(merged[u], 1)

                def step(g, u, n, m, k, prev, nxt):
                    add(u, n, 0)
                    add(u, n, 1)
                    dot(u, n, 0)
                    add(u, n, 2)
                    dot(u, n, 1)
                    if nxt:
                        if prev:
                            v.wait_ge(summed[1 - u], m)
                            v.nop(nofuse=True)
                        one_hot(g + 1, 1 - u)
                    add(u, n, 3)
                    dot(u, n, 2)
                    if prev:
                        merge(g - 1, 1 - u, m)
                    dot(u, n, 3)

                v.wait_ge(base_ready, p + 1)
                v.nop(nofuse=True)
                one_hot(0, 0)
                pipeline(v, p, step, merge)

            def update(l):
                with v.Fori(0, CB) as b:
                    n = l * CB + b + 1
                    for u in range(2):
                        v.wait_ge(u_new[u], n)
                        v.nop(nofuse=True)
                        h = chunk(hT, 2 * b + u)
                        v_.scalar_tensor_tensor(out=h, in0=bank[4 + u][:, 0:CH], scalar=gcol[:, :], in1=h,
                                                op0=ALU.add, op1=ALU.add).then_inc(u_h[u], 1)

            with v.Fori(0, LAYERS) as l:
                split(l, 2 * D, 2 * D)
                v.wait_ge(acc_zero, l + 1)
                v.nop(nofuse=True)
                all_rounds(l, lambda r: message_pass(l * R + r))
                update(l)

            def norm(q, b, into):
                for u in range(2):
                    v.wait_ge(n_mu[u], q)
                    v.nop(nofuse=True)
                    v_.tensor_tensor(t2[:, u, :], t1[:, u, :], bank[u][:, 0:CH], ALU.subtract).then_inc(n_d[u], 1)
                for u in range(2):
                    v.wait_ge(n_std[u], q)
                    v.nop(nofuse=True)
                    v_.reciprocal(t1[:, u, :], t3[:, u, :]).then_inc(n_r[u], 1)
                for u in range(2):
                    v.wait_ge(n_r[u], q)
                    v.nop(nofuse=True)
                    v_.tensor_tensor(into(u), t2[:, u, :], t1[:, u, :], ALU.mult).then_inc(n_x1[u], 1)
                v.wait_ge(n_x1[1], q)
                v.nop(nofuse=True)

            v.wait_ge(u_h[1], LAYERS * CB + 1)
            v.nop(nofuse=True)
            with v.Fori(0, CB) as b:
                for u in range(2):
                    v_.tensor_tensor(t1[:, u, :], chunk(hT, 2 * b + u), chunk(xT, 2 * b + u), ALU.add
                                     ).then_inc(n_y[u], 1)
                norm(b + 1, b, lambda u: chunk(hT, 2 * b + u))
            split(LAYERS, D + 1, D)

            def attention_pass(p, r):
                def dot(u, n, q):
                    v.wait_ge(picked[u][q], n)
                    v.nop(nofuse=True)
                    v.wait_ge(gathered[u][q], n * 32)
                    v.nop(nofuse=True)
                    for t in (2 * q, 2 * q + 1):
                        at = (t % 2) * 2 * D
                        ins = v_.scalar_tensor_tensor(out=junk[:, t, :], in0=bank[q % 2][:, at:at + D + 1], scalar=1.0,
                                                      in1=xrow[:, u, t, :], op0=ALU.mult, op1=ALU.mult,
                                                      accum_out=lg[:, u, t:t + 1])
                    ins.then_inc(dotted[u][q], 1)

                def node_max(u, n, a):
                    for h in range(2):
                        v.wait_ge(oht_ready[u][h], n)
                        v.nop(nofuse=True)
                    v.wait_ge(s_spread, a)
                    v.nop(nofuse=True)
                    v_.tensor_tensor_reduce(out=junkm[:, :], in0=score_ps, in1=mask[:, u, :], scale=1.0,
                                            scalar=-BIG / 2, op0=ALU.add, op1=ALU.max, accum_out=mloc[:, :]
                                            ).then_inc(s_max, 1)
                    v.wait_ge(s_max, a)
                    v.nop(nofuse=True)
                    v_.tensor_copy(m3[:, 0:1], mloc[:, :]).then_inc(s_hi, 1)
                    v.wait_ge(s_hi, a)
                    v.nop(nofuse=True)
                    v_.tensor_tensor(m3[:, 1:2], mloc[:, :], m3[:, 0:1], ALU.subtract)
                    v_.tensor_tensor(mres[:, :], mloc[:, :], m3[:, 0:1], ALU.subtract).then_inc(s_mid, 1)
                    v.wait_ge(s_mid, a)
                    v.nop(nofuse=True)
                    v_.tensor_tensor(m3[:, 2:3], mres[:, :], m3[:, 1:2], ALU.subtract).then_inc(s_lo, 1)

                def less_max(u, a):
                    v.wait_ge(s_me, a)
                    v.nop(nofuse=True)
                    v_.tensor_reduce(me[:, :], sc_me, AX.X, ALU.add).then_inc(s_mer, 1)
                    v.wait_ge(s_mer, a)
                    v.nop(nofuse=True)
                    v_.tensor_tensor(sm[:, :], lg[:, u, :], me[:, :], ALU.subtract).then_inc(s_sub, 1)

                def merge_max(g, u, a):
                    old = mrun[:, bass.ds(window(v, g), WIN)]
                    v_.tensor_tensor(mnew[:, :], sc_max, old, ALU.max).then_inc(s_mnew, 1)
                    v.wait_ge(s_mnew, a)
                    v.nop(nofuse=True)
                    v_.tensor_tensor(diff[:, 0, :], old, mnew[:, :], ALU.subtract)
                    v_.tensor_tensor(diff[:, 1, :], sc_max, mnew[:, :], ALU.subtract).then_inc(s_diff, 1)

                def merge(g, u, n):
                    a = group_tick(r, g)
                    row = window(v, g)
                    at = acc[:, :, bass.ds(row, WIN)]
                    v.wait_ge(s_ed, a)
                    v.nop(nofuse=True)
                    v.wait_ge(scat_done[u], n)
                    v.nop(nofuse=True)
                    v_.tensor_copy(mrun[:, bass.ds(row, WIN)], mnew[:, :])
                    v_.tensor_tensor(newsc[:, :, :], sc_sum[u], ed[:, 1:2, :].to_broadcast([P, 2, WIN]), ALU.mult)
                    v_.tensor_tensor(oldsc[:, :, :], at, ed[:, 0:1, :].to_broadcast([P, 2, WIN]), ALU.mult
                                     ).then_inc(s_scaled, 1)
                    v.wait_ge(s_scaled, a)
                    v.nop(nofuse=True)
                    v_.tensor_tensor(at, newsc[:, :, :], oldsc[:, :, :], ALU.add).then_inc(merged[u], 1)

                def step(g, u, n, m, k, prev, nxt):
                    a = group_tick(r, g)
                    dot(u, n, 0)
                    dot(u, n, 1)
                    if nxt:
                        if prev:
                            v.wait_ge(summed[1 - u], m)
                            v.nop(nofuse=True)
                        one_hot(g + 1, 1 - u)
                    dot(u, n, 2)
                    if prev:
                        merge(g - 1, 1 - u, m)
                    dot(u, n, 3)
                    node_max(u, n, a)
                    less_max(u, a)
                    merge_max(g, u, a)

                v.wait_ge(base_ready, p + 1)
                v.nop(nofuse=True)
                one_hot(0, 0)
                pipeline(v, p, step, merge)

            v.wait_ge(acc_zero, LAYERS + 2)
            v.nop(nofuse=True)
            all_rounds(LAYERS, lambda r: attention_pass(LAYERS * R + r, r))

            v.wait_ge(merged[1], (LAYERS + 1) * (R * BODIES))
            v.nop(nofuse=True)
            with v.Fori(0, CB) as b:
                n = b + 1
                for u in range(2):
                    v_.tensor_scalar(t1[:, u, :], acc[:, 1, bass.ds((2 * b + u) * CH, CH)], 1e-30, None, ALU.max
                                     ).then_inc(f_inv[u], 1)
                for u in range(2):
                    v.wait_ge(f_inv[u], 2 * b + 1)
                    v.nop(nofuse=True)
                    v_.reciprocal(t2[:, u, :], t1[:, u, :]).then_inc(f_inv[u], 1)
                for u in range(2):
                    v_.scalar_tensor_tensor(out=aggs[:, u, :], in0=acc[:, 1, bass.ds((2 * b + u) * CH, CH)], scalar=0.0,
                                            in1=chunk(hT, 2 * b + u), op0=ALU.is_le, op1=ALU.mult)
                for u in range(2):
                    v.wait_ge(f_inv[u], 2 * b + 2)
                    v.nop(nofuse=True)
                    v_.tensor_tensor(t1[:, u, :], acc[:, 0, bass.ds((2 * b + u) * CH, CH)], t2[:, u, :], ALU.mult
                                     ).then_inc(f_avg[u], 1)
                for u in range(2):
                    v.wait_ge(f_avg[u], n)
                    v.nop(nofuse=True)
                    v_.tensor_tensor(t1[:, u, :], t1[:, u, :], aggs[:, u, :], ALU.add).then_inc(f_sel[u], 1)
                for u in range(2):
                    v.wait_ge(f_o[u], n)
                    v.nop(nofuse=True)
                    v_.tensor_tensor(t1[:, u, :], t3[:, u, :], chunk(hT, 2 * b + u), ALU.add).then_inc(n_y[u], 1)
                norm(CB + n, b, lambda u: t3[:, u, :])

        @block.tensor
        def _(pe):
            mm, tr = nc.tensor.matmul, nc.tensor.transpose
            pe.wait_ge(loaded, 16 * LOADS)
            pe.nop(nofuse=True)
            pe.wait_ge(ident_done, 4)
            pe.nop(nofuse=True)
            pe.wait_ge(const_done, 2)
            pe.nop(nofuse=True)
            pe.wait_ge(setup_dve, 3)
            pe.nop(nofuse=True)
            mm(bank[2][0:1, 0:NG], rmin[:, :], ident[0:NG, 0:NG], start=True, stop=True)
            mm(bank[2][0:1, NG:2 * NG], span[:, :], ident[0:NG, 0:NG], start=True, stop=True)
            mm(bank[2][:, 2 * NG:3 * NG], rmin[:, 0:1].to_broadcast([NG, P]), ident[0:NG, 0:NG],
               start=True, stop=True).then_inc(setup_pe, 1)
            tr(bank[3][:, P:2 * P], Wk[:, :], ident[:, :]).then_inc(setup_pe, 1)
            pe.wait_ge(loaded_tail, 16)
            pe.nop(nofuse=True)
            for k, first in enumerate(GROUPS4):
                if k >= 2:
                    pe.wait_ge(xt_done, k - 1)
                    pe.nop(nofuse=True)
                for t in range(first, min(first + 4, NT)):
                    ins = tr(bank[k % 2][:, (t - first) * P:(t - first + 1) * P], xN[:, t, :], ident[:, :])
                ins.then_inc(xt_ps, 1)
            pe.wait_ge(setup_dve, 8)
            pe.nop(nofuse=True)
            mm(bank[3][:, 0:1], glbW[:, :], col(SUMX), start=True, stop=True).then_inc(setup_pe, 1)
            R = rounds(pe)

            def tables(q, product):
                with pe.Fori(0, TB) as b:
                    n = q * TB + b + 1
                    for u in range(2):
                        pe.wait_ge(staged[u], n)
                        pe.nop(nofuse=True)
                        pe.wait_ge(res_done[u], n)
                        pe.nop(nofuse=True)
                        product(u).then_inc(tab_ps[u], 1)

            def message_rows(u):
                mm(bank[u], stage[:, u, 0, :], wcat[:, :], start=True, stop=False)
                return mm(bank[u][:, 2 * D:4 * D], ones[0:1, :], b1row[0:1, :], start=False, stop=True)

            def attention_rows(u):
                tr(bank[u][:, 0:D], stage[:, u, 0, :], ident[:, :])
                return mm(bank[u][:, D:2 * D + 1], stage[:, u, 1, :], WkTb[:, :], start=True, stop=True)

            def turn(u, n):
                pe.wait_ge(oh_ready[u], n)
                pe.nop(nofuse=True)
                for h in range(2):
                    for t in range(4):
                        ins = tr(ohp[h][0:3 * WIN, t * P:(t + 1) * P], oh[:, u, 4 * h + t, :], ident[:, :])
                    ins.then_inc(ohp_ready[u][h], 1)

            def pick(u, q, into, win, width):
                for t in (2 * q, 2 * q + 1):
                    at = (t % 2) * 2 * D
                    ins = mm(into[:, at:at + width], oht[:, u, t * P:(t + 1) * P], win[:, u, :], start=True, stop=True)
                return ins

            def scatter(u, n):
                pe.wait_ge(zw_ready[u], n)
                pe.nop(nofuse=True)
                for t in range(TG):
                    ins = mm(scat[u][0:WIN, 0:D + 1], oh[:, u, t, 0:WIN], zw[:, u, t, :],
                             start=(t == 0), stop=(t == TG - 1))
                ins.then_inc(summed[u], 1)

            def turn_sums(u, n):
                pe.wait_ge(sum_out[u], n)
                pe.nop(nofuse=True)
                tr(sc_sum[u][:, 0, :], ssum[:, u, 0:D], ident[0:WIN, 0:WIN])
                tr(sc_sum[u][:, 1, :], ssum[:, u, D:D + 1].to_broadcast([WIN, P]), ident[0:WIN, 0:WIN]
                   ).then_inc(scat_done[u], 1)

            def last_sums(g, u, n):
                scatter(u, n)
                turn_sums(u, n)

            def message_pass(p):
                def rows(u, n, m, q):
                    if q == 0:
                        pe.wait_ge(win_ld[u], n * 48)
                        pe.nop(nofuse=True)
                    pe.wait_ge(oht_ready[u][q // 2], n)
                    pe.nop(nofuse=True)
                    pe.wait_ge(added[1 - u][q], m + 1)
                    pe.nop(nofuse=True)
                    pick(u, q, bank[q], bwin, 2 * D).then_inc(picked[u][q], 1)

                def step(g, u, n, m, k, prev, nxt):
                    rows(u, n, m, 0)
                    rows(u, n, m, 1)
                    if prev:
                        scatter(1 - u, m)
                    rows(u, n, m, 2)
                    rows(u, n, m, 3)
                    if prev:
                        turn_sums(1 - u, m)
                    if nxt:
                        turn(1 - u, k)

                turn(0, p * BODIES + 1)
                pipeline(pe, p, step, last_sums)

            def update(l):
                pe.wait_ge(merged[1], (l + 1) * (R * BODIES))
                pe.nop(nofuse=True)
                with pe.Fori(0, CB) as b:
                    n = l * CB + b + 1
                    for u in range(2):
                        at = bass.ds((2 * b + u) * CH, CH)
                        mm(bank[u][:, 0:CH], msgW2[:, :], acc[:, 0, at], start=True, stop=False)
                        mm(bank[u][:, 0:CH], b2row[0:1, :], acc[0:1, 1, at], start=False, stop=True
                           ).then_inc(u_agg[u], 1)
                    for u in range(2):
                        mm(bank[2 + u][:, 0:CH], updW1[:, 0, :], chunk(hT, 2 * b + u), start=True, stop=False)
                        pe.wait_ge(u_aggc[u], n)
                        pe.nop(nofuse=True)
                        mm(bank[2 + u][:, 0:CH], updW1[:, 1, :], aggs[:, u, :], start=False, stop=True
                           ).then_inc(u_hid[u], 1)
                    for u in range(2):
                        pe.wait_ge(u_relu[u], n)
                        pe.nop(nofuse=True)
                        pe.wait_ge(u_h[u], n)
                        pe.nop(nofuse=True)
                        mm(bank[4 + u][:, 0:CH], updW2[:, :], hid[:, u, :], start=True, stop=True
                           ).then_inc(u_new[u], 1)

            with pe.Fori(0, LAYERS) as l:
                tables(l, message_rows)
                with pe.Fori(0, R) as r:
                    message_pass(l * R + r)
                update(l)

            def norm(q):
                for u in range(2):
                    pe.wait_ge(n_y[u], q)
                    pe.nop(nofuse=True)
                    mm(bank[u][:, 0:CH], inv_d[:, :], t1[:, u, :], start=True, stop=True).then_inc(n_mu[u], 1)
                for u in range(2):
                    pe.wait_ge(n_sq[u], q)
                    pe.nop(nofuse=True)
                    mm(bank[2 + u][:, 0:CH], inv_d[:, :], t3[:, u, :], start=True, stop=True).then_inc(n_var[u], 1)

            with pe.Fori(0, CB) as b:
                norm(b + 1)
                for u in range(2):
                    pe.wait_ge(n_x1[u], b + 1)
                    pe.nop(nofuse=True)
                    mm(bank[4 + u][:, 0:CH], Wq[:, :], chunk(hT, 2 * b + u), start=True, stop=True
                       ).then_inc(n_lin[u], 1)
            tables(LAYERS, attention_rows)

            def attention_pass(p, r):
                def rows(u, n, q):
                    if q == 0:
                        pe.wait_ge(win_ld[u], n * 48)
                        pe.nop(nofuse=True)
                    if q >= 2:
                        pe.wait_ge(dotted[u][q - 2], n)
                        pe.nop(nofuse=True)
                    pe.wait_ge(oht_ready[u][q // 2], n)
                    pe.nop(nofuse=True)
                    pick(u, q, bank[q % 2], qwin, D + 1).then_inc(picked[u][q], 1)

                def spread(u, n, q):
                    pe.wait_ge(dotted[u][q], n)
                    pe.nop(nofuse=True)
                    for t in (2 * q, 2 * q + 1):
                        ins = tr(score_ps[:, t * P:(t + 1) * P], lg[:, u, t:t + 1].to_broadcast([P, WIN]), ident[:, :])
                    return ins

                def step(g, u, n, m, k, prev, nxt):
                    a = group_tick(r, g)
                    rows(u, n, 0)
                    rows(u, n, 1)
                    if prev:
                        scatter(1 - u, m)
                    spread(u, n, 0)
                    rows(u, n, 2)
                    spread(u, n, 1)
                    if prev:
                        turn_sums(1 - u, m)
                    rows(u, n, 3)
                    spread(u, n, 2)
                    spread(u, n, 3).then_inc(s_spread, 1)
                    if nxt:
                        turn(1 - u, k)
                    pe.wait_ge(s_lo, a)
                    pe.nop(nofuse=True)
                    for t in range(TG):
                        mm(sc_me[:, t, :], oht[0:WIN, u, t * P:(t + 1) * P], m3[:, :], start=True, stop=True)
                    tr(sc_max, mloc[:, 0:1].to_broadcast([WIN, P]), ident[0:WIN, 0:WIN]).then_inc(s_me, 1)

                turn(0, p * BODIES + 1)
                pipeline(pe, p, step, last_sums)

            with pe.Fori(0, R) as r:
                attention_pass(LAYERS * R + r, r)

            with pe.Fori(0, CB) as b:
                n = b + 1
                for u in range(2):
                    pe.wait_ge(f_sel[u], n)
                    pe.nop(nofuse=True)
                    mm(bank[u][:, 0:CH], Wv[:, :], t1[:, u, :], start=True, stop=True).then_inc(n_lin[u], 1)
                for u in range(2):
                    pe.wait_ge(n_linc[u], CB + n)
                    pe.nop(nofuse=True)
                    mm(bank[2 + u][:, 0:CH], Wl[:, :], t2[:, u, :], start=True, stop=True).then_inc(f_l[u], 1)
                norm(CB + n)
                for u in range(2):
                    pe.wait_ge(n_x1[u], CB + n)
                    pe.nop(nofuse=True)
                    for k in range(4):
                        ins = tr(bank[4 + u][0:PIECE, k * D:(k + 1) * D], t3[:, u, k * PIECE:(k + 1) * PIECE],
                                 ident[:, :])
                    ins.then_inc(f_t[u], 1)


_GNN = ("msg_W1", "msg_b1", "msg_W2", "msg_b2", "upd_W1", "upd_b1", "upd_W2", "upd_b2",
        "att_W1", "att_b1", "att_W2", "att_b2", "glb_W", "glb_b")
_ATT = ("Wq", "bq", "Wk", "bk", "Wv", "bv", "Wl", "bl")


def kernel(**inputs):
    import concourse.bacc as bacc
    from concourse.bass_utils import run_bass_kernel_spmd

    def padded(name, fill):
        a = np.full((NG * TG * P,), fill, np.int32)
        a[:E] = np.asarray(inputs[name])
        return a.reshape(NG, TG, P)

    src, dst = padded("src", 0), padded("dst", N)
    arrays = {
        "x": np.ascontiguousarray(inputs["x"]),
        "idx": np.ascontiguousarray(src.transpose(0, 2, 1)).reshape(NG * P, TG),
        "dst_pm": np.ascontiguousarray(dst.transpose(2, 0, 1)).reshape(P, NG * TG),
        "dst_gm": dst.reshape(NG, TG * P),
    }
    for prefix, names in (("L0_gnn_", _GNN), ("L1_gnn_", _ATT)):
        for n in names:
            arrays[n] = np.ascontiguousarray(inputs[prefix + n])
    nc = bacc.Bacc("TRN2", target_bir_lowering=False, num_devices=1)
    aps = {n: nc.dram_tensor(f"in_{n}", a.shape, mybir.dt.from_np(a.dtype), kind="ExternalInput").ap()
           for n, a in arrays.items()}
    out = nc.dram_tensor("out_0", (N, D), F32, kind="ExternalOutput").ap()
    build(nc, aps["x"], aps["idx"], aps["dst_pm"], aps["dst_gm"], aps, out)
    r = run_bass_kernel_spmd(nc, [{f"in_{n}": a for n, a in arrays.items()}], core_ids=[0])
    return r.results[0]["out_0"]
```

```python
import concourse.bass as bass
import concourse.mybir as mybir
import numpy as np
from contextlib import ExitStack

F32, BF16, I32 = mybir.dt.float32, mybir.dt.bfloat16, mybir.dt.int32
ALU, ACT, AX = mybir.AluOpType, mybir.ActivationFunctionType, mybir.AxisListType

P = 128
N, E, D = 3125, 100000, 128
NT = 26
NPAD = NT * P
CH = NPAD // 8
TG = 8
NG = 98
BODIES = NG // 2
WIN = 42
PAIRS = TG // 2
LAYERS = 2
SLOTS = 4
ROUNDS = -(-(N + 1) // WIN)
BIG = 3.0e38
PIECE = CH // 4
EPS = 1e-5


def build(nc, x, idx, dst_pm, dst_gm, w, out):
    A_tab = nc.dram_tensor("A_tab", (NPAD, 2 * D), F32, kind="Internal").ap()
    B_tab = nc.dram_tensor("B_tab", (NPAD, 3 * 2 * D), BF16, kind="Internal").ap()
    X_tab = nc.dram_tensor("X_tab", (NPAD, D), F32, kind="Internal").ap()
    Q_tab = nc.dram_tensor("Q_tab", (NPAD, 3 * (D + 1)), BF16, kind="Internal").ap()

    with ExitStack() as ctx:
        def sb(name, shape, dt=F32):
            return ctx.enter_context(nc.sbuf_tensor(name, shape, dt))

        def pb(name, shape, dt=F32):
            return ctx.enter_context(nc.psum_tensor(name, shape, dt))

        def sem(name):
            return ctx.enter_context(nc.semaphore(name))

        def sems(name, *dims):
            if not dims:
                return sem(name)
            return [sems(f"{name}_{k}", *dims[1:]) for k in range(dims[0])]

        hT = sb("hT", [P, NPAD])
        xT = sb("xT", [P, NPAD])
        xN = sb("xN", [P, NT, D])
        acc = sb("acc", [P, 2, NPAD])
        mrun = sb("mrun", [P, NPAD])
        ident = sb("ident", [P, P])
        inv_d = sb("inv_d", [P, P])
        iota_w = sb("iota_w", [P, 3, WIN])
        ident16 = sb("ident16", [P, P], BF16)
        iota16 = sb("iota16", [P, 3 * WIN], BF16)
        rel16 = sb("rel16", [P, NG * TG], BF16)
        eps_c = sb("eps_c", [P, 1])
        dstI = sb("dstI", [P, NG * TG], I32)
        dst0 = sb("dst0", [P, NG * TG])
        dst_rel = sb("dst_rel", [P, NG * TG])
        rowsI = sb("rowsI", [NG, TG * P], I32)
        rmin = sb("rmin", [NG, 1])
        rmax = sb("rmax", [NG, 1])
        span = sb("span", [NG, 1])
        base0 = sb("base0", [1, NG])
        baseF = sb("baseF", [1, NG])
        baseI = sb("baseI", [1, NG], I32)
        spanm = sb("spanm", [1, 1])
        steps = sb("steps", [1, ROUNDS])
        within = sb("within", [1, ROUNDS])
        count = sb("count", [1, 1])
        roundsI = sb("roundsI", [1, 1], I32)
        wcat = sb("wcat", [P, 4 * D])
        b1parts = sb("b1parts", [P, 2 * D], BF16)
        ones16 = sb("ones16", [P, P], BF16)
        attw = sb("attw", [P, D])
        attb = sb("attb", [P, 1])
        msgW2 = sb("msgW2", [P, D])
        msgW2T = sb("msgW2T", [P, D])
        msg_upd = sb("msg_upd", [P, D])
        updW1 = sb("updW1", [P, 2, D])
        updW2 = sb("updW2", [P, D])
        glbW = sb("glbW", [P, D])
        Wq = sb("Wq", [P, D])
        Wk = sb("Wk", [P, D])
        WkTb = sb("WkTb", [P, D + 1])
        Wv = sb("Wv", [P, D])
        Wl = sb("Wl", [P, D])
        cols = sb("cols", [P, 10])
        UB1, UB2, GLB, BQ, BV, BL, SUMX, GH, B2, B2U = range(10)
        gcol = sb("gcol", [P, 1])

        def col(k):
            return cols[:, k:k + 1]

        idx_st = sb("idx_st", [P, 2, TG], I32)
        rows_sb = sb("rows_sb", [P, SLOTS * TG * (D + 1)])
        arow = rows_sb[:, 0:2 * TG * 2 * D].rearrange("p (u t d) -> p u t d", u=2, t=TG)
        xrow = rows_sb[:, :].rearrange("p (s t d) -> p s t d", s=SLOTS, t=TG)
        bwin = sb("bwin", [3 * WIN, 2, 2 * D], BF16)
        qwin = sb("qwin", [3 * WIN, 2, D + 1], BF16)
        oh = sb("oh", [P, 2, TG, 3 * WIN], BF16)
        oht = sb("oht", [3 * WIN, 2, TG * P], BF16)
        mask = sb("mask", [WIN, 2, TG * P], BF16)
        pre = sb("pre", [P, 2, TG, 2 * D])
        ohw = sb("ohw", [P, 2, TG, WIN])
        relu = sb("relu", [P, 2, TG, D + 1])
        junk = sb("junk", [P, TG, D + 1], BF16)
        junkm = sb("junkm", [WIN, TG * P], BF16)
        lg = sb("lg", [P, 2, TG])
        wt = sb("wt", [P, 2, TG])
        sm = sb("sm", [P, TG])
        ssum = sb("ssum", [WIN, 2, D + 1])
        me = sb("me", [P, TG])
        mloc = sb("mloc", [WIN, 1])
        mres = sb("mres", [WIN, 1])
        m3 = sb("m3", [WIN, 3], BF16)
        mnew = sb("mnew", [P, WIN])
        diff = sb("diff", [P, 2, WIN])
        ed = sb("ed", [P, 2, 2, WIN])
        newsc = sb("newsc", [P, 2, WIN])
        oldsc = sb("oldsc", [P, 2, WIN])
        stage = sb("stage", [P, 2, 2, P])
        tabA = sb("tabA", [P, 2, 2 * D])
        tabB = sb("tabB", [P, 2, 3, 2 * D], BF16)
        res = sb("res", [P, 2, 2 * D])
        aggs = sb("aggs", [P, 2, CH])
        hid = sb("hid", [P, 2, CH])
        t1 = sb("t1", [P, 2, CH])
        t2 = sb("t2", [P, 2, CH])
        t3 = sb("t3", [P, 2, CH])
        outn = sb("outn", [PIECE, 2, 4, D])


        psum = pb("psum_main", [P, 6 * 512])
        bank = [psum[:, k * 512:(k + 1) * 512] for k in range(6)]
        scat = [pb(f"scat{k}", [P, 512]) for k in range(2)]
        bg = [bank[k].rearrange("p (t n) -> p t n", t=2) for k in range(4)]
        ohp = [bank[4 + u].bitcast(BF16) for u in range(2)]
        score_ps = psum[0:WIN, 2 * 512:4 * 512]
        sc_sum = [scat[k][:, 256:256 + 2 * WIN].rearrange("p (a n) -> p a n", a=2) for k in range(2)]
        sc_max = bank[2][:, 0:WIN]
        sc_me = bank[2][:, WIN:WIN + 3 * TG].rearrange("p (t k) -> p t k", k=3)

        loaded, loaded_tail = sem("loaded"), sem("loaded_tail")
        const_done = sem("const_done")
        ident_done = sem("ident_done")
        setup_dve, setup_pe, setup_act = sem("setup_dve"), sem("setup_pe"), sem("setup_act")
        xt_ps, xt_done = sem("xt_ps"), sem("xt_done")
        ready_all = sem("ready_all")
        moved = sem("moved")
        base_ready = sem("base_ready")
        acc_zero = sem("acc_zero")
        staged, tab_ps, a_copied, hi_done, res_done, mid_done, lo_done, a_out, b_out = (sems(n, 2) for n in (
            "staged", "tab_ps", "a_copied", "hi_done", "res_done", "mid_done", "lo_done", "a_out", "b_out"))
        idx_ld, win_ld = sems("idx_ld", 2), sems("win_ld", 2)
        gathered = sems("gathered", 2, PAIRS)
        oh_ready, ohp_ready, oht_ready, mask_ready = sems("oh_ready", 2), sems("ohp_ready", 2), sems("oht_ready", 2, 2), sem("mask_ready")
        picked, dotted = sems("picked", 2, PAIRS), sems("dotted", 2, PAIRS)
        added = sems("added", 2, PAIRS)
        wt_ready, ohw_ready, summed, sum_out, scat_done, merged = (sems(n, 2) for n in (
            "wt_ready", "ohw_ready", "summed", "sum_out", "scat_done", "merged"))
        u_lin, u_pre, u_relu, u_new, u_h = (sems(n, 2) for n in ("u_lin", "u_pre", "u_relu", "u_new", "u_h"))
        n_y, n_mu, n_d, n_sq, n_var, n_std, n_r, n_x1, n_lin, n_linc = (sems(n, 2) for n in (
            "n_y", "n_mu", "n_d", "n_sq", "n_var", "n_std", "n_r", "n_x1", "n_lin", "n_linc"))
        (s_spread, s_max, s_hi, s_mid, s_lo, s_me, s_mer, s_sub, s_mnew, s_diff, s_ed, s_scaled) = (
            sem(n) for n in ("s_spread", "s_max", "s_hi", "s_mid", "s_lo", "s_me", "s_mer", "s_sub",
                             "s_mnew", "s_diff", "s_ed", "s_scaled"))
        f_inv, f_avg, f_sel, f_l, f_o, f_t, f_n = (sems(n, 2) for n in (
            "f_inv", "f_avg", "f_sel", "f_l", "f_o", "f_t", "f_n"))
        out_sem = sems("out_sem", 2)

        block = ctx.enter_context(nc.Block())
        LOADS = 27
        FULL, REST = N // P, N % P
        TB = NT // 2
        CB = NPAD // CH // 2
        GROUPS4 = list(range(0, NT, 4))

        def rounds(eng):
            eng.wait_ge(ready_all, 1)
            eng.nop(nofuse=True)
            return eng.value_load(roundsI[0:1, 0:1], min_val=1, max_val=ROUNDS)

        def window(eng, g):
            return eng.value_load(baseI[0:1, bass.ds(g, 1)], min_val=0, max_val=NPAD - WIN)

        def chunk(t, c):
            return t[:, bass.ds(c * CH, CH)]

        def group_tick(r, g):
            return r * NG + g + 1

        def ticks(p, body, g):
            return p * BODIES + body * (SLOTS // 2) + g // 2 + 1

        def pipeline(eng, p, step, tail):
            def one(body, g, prev=True, nxt=True):
                step(SLOTS * body + g, g % SLOTS, ticks(p, body, g), ticks(p, body, g - 1), ticks(p, body, g + 1), prev, nxt)

            one(0, 0, prev=False)
            with eng.Fori(0, (NG - 2) // SLOTS) as body:
                for g in range(1, SLOTS + 1):
                    one(body, g)
            last = NG - 1
            one(last // SLOTS, last % SLOTS, nxt=False)
            tail(last, last % SLOTS, ticks(p, 0, last))

        @block.sync
        def _(sp):
            def load(dst, src):
                sp.dma_start(dst, src).then_inc(loaded, 16)

            load(xN[:, 0:FULL, :], x[0:FULL * P, :].rearrange("(t p) d -> p t d", p=P))
            load(rowsI[:, :], dst_gm)
            load(dstI[:, :], dst_pm)
            for k, (name, half) in enumerate((("msg_W1", 0), ("att_W1", 0), ("msg_W1", 1), ("att_W1", 1))):
                load(wcat[:, k * D:(k + 1) * D], w[name][half * D:(half + 1) * D, :])
            for k, name in enumerate(("msg_b1", "att_b1")):
                load(tabA[:, 0, k * D:(k + 1) * D], w[name].rearrange("(a d) -> a d", a=1).broadcast_to([P, D]))
            for dst, name in ((msgW2, "msg_W2"), (updW2, "upd_W2"), (glbW, "glb_W"), (Wq, "Wq"), (Wk, "Wk"),
                              (Wv, "Wv"), (Wl, "Wl")):
                load(dst[:, :], w[name])
            load(updW1[:, :, :], w["upd_W1"].rearrange("(a k) n -> k a n", a=2))
            load(attw[:, :], w["att_W2"].rearrange("d a -> a d").broadcast_to([P, D]))
            load(attb[:, :], w["att_b2"].rearrange("(a d) -> a d", a=1).broadcast_to([P, 1]))
            load(WkTb[:, D:D + 1], w["bk"].rearrange("(p a) -> p a", a=1))
            for k, name in ((UB1, "upd_b1"), (UB2, "upd_b2"), (GLB, "glb_b"), (BQ, "bq"), (BV, "bv"), (BL, "bl"),
                            (B2, "msg_b2")):
                load(col(k), w[name].rearrange("(p a) -> p a", a=1))
            sp.wait_ge(const_done, 1)
            sp.nop(nofuse=True)
            sp.dma_start(xN[0:REST, FULL, :], x[FULL * P:N, :]).then_inc(loaded_tail, 16)
            for s in (a_out, b_out):
                for u in range(2):
                    sp.sem_inc(s[u], 16)
            for u in range(2):
                sp.sem_inc(out_sem[u], 64)
            R = rounds(sp)

            def one_pass(p, win, tab):
                sp.wait_ge(base_ready, p + 1)
                sp.nop(nofuse=True)

                width = win.shape[2]

                def step(g, u, ticks):
                    if ticks is not None:
                        for q in range(PAIRS):
                            sp.wait_ge(gathered[u][q], ticks * 32)
                            sp.nop(nofuse=True)
                    sp.dma_start(idx_st[:, u, :], idx[bass.ds(g * P, P), :]).then_inc(idx_ld[u], 16)
                    row = window(sp, g)
                    if ticks is not None:
                        sp.wait_ge(picked[u][PAIRS - 1], ticks)
                        sp.nop(nofuse=True)
                    for k in range(3):
                        sp.dma_start(win[k * WIN:(k + 1) * WIN, u, :],
                                     tab[bass.ds(row, WIN), k * width:(k + 1) * width]).then_inc(win_ld[u], 16)

                step(0, 0, None)
                step(1, 1, None)
                with sp.Fori(1, BODIES) as j:
                    step(2 * j, 0, p * BODIES + j)
                    step(2 * j + 1, 1, p * BODIES + j)

            def store_tables(q, rows, row_n, parts, parts_n):
                with sp.Fori(0, TB) as b:
                    for u in range(2):
                        n = q * TB + b + 1
                        at = bass.ds((2 * b + u) * P, P)
                        sp.wait_ge(a_copied[u], n)
                        sp.nop(nofuse=True)
                        sp.dma_start(rows[at, :], tabA[:, u, 0:row_n]).then_inc(a_out[u], 16)
                        sp.wait_ge(lo_done[u], n)
                        sp.nop(nofuse=True)
                        sp.dma_start(parts[at, :].rearrange("p (k d) -> p k d", k=3),
                                     tabB[:, u, :, 0:parts_n]).then_inc(b_out[u], 16)
                for u in range(2):
                    sp.wait_ge(b_out[u], (q + 1) * (TB * 16) + 16)
                    sp.nop(nofuse=True)

            with sp.Fori(0, LAYERS) as l:
                store_tables(l, A_tab, 2 * D, B_tab, 2 * D)
                with sp.Fori(0, R) as r:
                    one_pass(l * R + r, bwin, B_tab)
            store_tables(LAYERS, X_tab, D, Q_tab, D + 1)
            with sp.Fori(0, R) as r:
                one_pass(LAYERS * R + r, qwin, Q_tab)

            def store_out(c, u, n, known):
                sp.wait_ge(f_n[u], n)
                sp.nop(nofuse=True)
                for k in range(4):
                    m = PIECE if known is None else min(PIECE, N - known * CH - k * PIECE)
                    if m > 0:
                        at = c * CH + k * PIECE
                        rows = bass.ds(at, PIECE) if known is None else slice(at, at + m)
                        sp.dma_start(out[rows, :], outn[0:m, u, k, :]).then_inc(out_sem[u], 16)

            with sp.Fori(0, CB - 1) as b:
                store_out(2 * b, 0, b + 1, None)
                store_out(2 * b + 1, 1, b + 1, None)
            last = 2 * (CB - 1)
            store_out(last, 0, CB, last)
            store_out(last + 1, 1, CB, last + 1)
            for u in range(2):
                pieces = sum(min(4, max(0, -(-(N - c * CH) // PIECE))) for c in range(u, 2 * CB, 2))
                sp.wait_ge(out_sem[u], 64 + 16 * pieces)
                sp.nop(nofuse=True)

        @block.gpsimd
        def _(pool):
            nc.gpsimd.memset(ident[:, :], 0.0).then_inc(ident_done, 1)
            nc.gpsimd.iota(iota_w[:, :, :], pattern=[[0, 3], [1, WIN]], base=0, channel_multiplier=0,
                           allow_small_or_imprecise_dtypes=True).then_inc(ident_done, 1)
            nc.gpsimd.iota(steps[:, :], pattern=[[WIN, ROUNDS]], base=0, channel_multiplier=0,
                           allow_small_or_imprecise_dtypes=True).then_inc(ident_done, 1)
            pool.wait_ge(ident_done, 3)
            pool.nop(nofuse=True)
            nc.gpsimd.affine_select(out=ident[:, :], in_=ident[:, :], compare_op=ALU.not_equal, fill=1.0,
                                    base=0, pattern=[[-1, P]], channel_multiplier=1).then_inc(ident_done, 1)
            R = rounds(pool)

            def wait_for_table(q):
                for u in range(2):
                    pool.wait_ge(a_out[u], (q + 1) * (TB * 16) + 16)
                    pool.nop(nofuse=True)

            def fetch(u, t, row, tab):
                nc.gpsimd.indirect_dma_start(
                    row, None, tab,
                    bass.IndirectOffsetOnAxis(ap=idx_st[:, u, t:t + 1], axis=0)).then_inc(gathered[u][t // 2], 16)

            def gather_a(p):
                with pool.Fori(0, BODIES) as j:
                    n = p * BODIES + j + 1
                    for u in range(2):
                        pool.wait_ge(idx_ld[u], n * 16)
                        pool.nop(nofuse=True)
                        for t in range(TG):
                            if t % 2 == 0:
                                pool.wait_ge(added[u][t // 2], n)
                                pool.nop(nofuse=True)
                            fetch(u, t, arow[:, u, t, :], A_tab)

            def gather_x(p):
                def group(s, n):
                    u = s % 2
                    pool.wait_ge(idx_ld[u], n * 16)
                    pool.nop(nofuse=True)
                    pool.wait_ge(summed[u], n)
                    pool.nop(nofuse=True)
                    for t in range(TG):
                        fetch(u, t, xrow[:, s, t, 0:D], X_tab)

                with pool.Fori(0, NG // SLOTS) as body:
                    for g in range(SLOTS):
                        group(g, ticks(p, body, g))
                for g in range(NG // SLOTS * SLOTS, NG):
                    group(g % SLOTS, ticks(p, 0, g))

            with pool.Fori(0, LAYERS) as l:
                pool.wait_ge(u_h[1], l * CB + 1)
                pool.nop(nofuse=True)
                nc.gpsimd.memset(acc[:, :, :], 0.0).then_inc(acc_zero, 1)
                wait_for_table(l)
                with pool.Fori(0, R) as r:
                    gather_a(l * R + r)
            pool.wait_ge(u_h[1], LAYERS * CB + 1)
            pool.nop(nofuse=True)
            nc.gpsimd.memset(acc[:, :, :], 0.0).then_inc(acc_zero, 1)
            nc.gpsimd.memset(mrun[:, :], -BIG / 2).then_inc(acc_zero, 1)
            nc.gpsimd.memset(xrow[:, :, :, D:D + 1], 1.0).then_inc(acc_zero, 1)
            wait_for_table(LAYERS)
            with pool.Fori(0, R) as r:
                gather_x(LAYERS * R + r)

        @block.scalar
        def _(act):
            for k, first in enumerate(GROUPS4):
                m = min(4, NT - first)
                act.wait_ge(xt_ps, k + 1)
                act.nop(nofuse=True)
                nc.scalar.copy(xT[:, first * P:(first + m) * P], bank[k % 2][:, 0:m * P]).then_inc(xt_done, 1)
            act.wait_ge(setup_pe, 3)
            act.nop(nofuse=True)
            nc.scalar.activation(col(GH), bank[3][:, 0:1], ACT.Relu, bias=col(GLB)).then_inc(setup_act, 1)
            R = rounds(act)

            def tables(q, width, b_at, a_width, with_q):
                def stage_tile(b, u):
                    at = bass.ds((2 * b + u) * P, P)
                    if with_q:
                        nc.scalar.copy(stage[:, u, 1, :], xT[:, at])
                    nc.scalar.copy(stage[:, u, 0, :], hT[:, at]).then_inc(staged[u], 1)

                def body(b, nxt):
                    n = q * TB + b + 1
                    for u in range(2):
                        act.wait_ge(tab_ps[u], n)
                        act.nop(nofuse=True)
                        if nxt:
                            stage_tile(b + 1, u)
                        act.wait_ge(a_out[u], n * 16)
                        act.nop(nofuse=True)
                        nc.scalar.copy(tabA[:, u, 0:a_width], bank[u][:, 0:a_width]).then_inc(a_copied[u], 1)
                        act.wait_ge(b_out[u], n * 16)
                        act.nop(nofuse=True)
                        nc.scalar.copy(tabB[:, u, 0, 0:width], bank[u][:, b_at:b_at + width]).then_inc(hi_done[u], 1)

                for u in range(2):
                    stage_tile(0, u)
                with act.Fori(0, TB - 1) as b:
                    body(b, True)
                body(TB - 1, False)

            def transposed(u, n, masked):
                act.wait_ge(ohp_ready[u], n)
                act.nop(nofuse=True)
                for h in range(2):
                    part = slice(h * 512, (h + 1) * 512)
                    nc.scalar.copy(oht[:, u, part], ohp[u][0:3 * WIN, part]).then_inc(oht_ready[u][h], 1)
                if masked:
                    nc.scalar.activation(mask[:, u, :], ohp[u][0:WIN, :], ACT.Copy, scale=BIG / 2, bias=-BIG / 2
                                         ).then_inc(mask_ready, 1)

            def sums_out(u, n):
                act.wait_ge(summed[u], n + SLOTS // 2)
                act.nop(nofuse=True)
                nc.scalar.copy(ssum[:, u, :], scat[u][0:WIN, 0:D + 1]).then_inc(sum_out[u], 1)

            def message_pass(p):
                def step(g, s, n, m, k, prev, nxt):
                    u = s % 2
                    for q in range(PAIRS):
                        two = slice(2 * q, 2 * q + 2)
                        act.wait_ge(added[u][q], n + 1)
                        act.nop(nofuse=True)
                        nc.scalar.activation(relu[:, u, two, 0:D], pre[:, u, two, 0:D], ACT.Relu)
                        if q == PAIRS - 1 and prev:
                            sums_out(1 - u, m)
                    if nxt:
                        transposed(1 - u, k, False)
                    act.wait_ge(dotted[u][PAIRS - 1], n)
                    act.nop(nofuse=True)
                    nc.scalar.activation(wt[:, u, :], lg[:, u, :], ACT.Sigmoid, bias=attb[:, :]).then_inc(wt_ready[u], 1)

                transposed(0, ticks(p, 0, 0), False)
                pipeline(act, p, step, lambda g, s, n: sums_out(s % 2, n))

            def update(l):
                with act.Fori(0, CB) as b:
                    n = l * CB + b + 1
                    for u in range(2):
                        act.wait_ge(u_pre[u], n)
                        act.nop(nofuse=True)
                        nc.scalar.activation(hid[:, u, :], t1[:, u, :], ACT.Relu, bias=col(UB1)).then_inc(u_relu[u], 1)

            with act.Fori(0, LAYERS) as l:
                act.wait_ge(u_h[1], l * CB + 1)
                act.nop(nofuse=True)
                tables(l, 2 * D, 2 * D, 2 * D, False)
                with act.Fori(0, R) as r:
                    message_pass(l * R + r)
                update(l)

            def norm(q):
                for u in range(2):
                    act.wait_ge(n_d[u], q)
                    act.nop(nofuse=True)
                    nc.scalar.activation(t3[:, u, :], t2[:, u, :], ACT.Square).then_inc(n_sq[u], 1)
                for u in range(2):
                    act.wait_ge(n_var[u], q)
                    act.nop(nofuse=True)
                    nc.scalar.activation(t3[:, u, :], bank[2 + u][:, 0:CH], ACT.Sqrt,
                                         bias=eps_c[:, :]).then_inc(n_std[u], 1)

            with act.Fori(0, CB) as b:
                norm(b + 1)
                for u in range(2):
                    act.wait_ge(n_lin[u], b + 1)
                    act.nop(nofuse=True)
                    nc.scalar.activation(chunk(xT, 2 * b + u), bank[4 + u][:, 0:CH], ACT.Identity,
                                         bias=col(BQ)).then_inc(n_linc[u], 1)
            act.wait_ge(n_x1[1], CB)
            act.nop(nofuse=True)
            for u in range(2):
                act.wait_ge(n_linc[u], CB)
                act.nop(nofuse=True)
            tables(LAYERS, D + 1, D, D, True)

            def attention_pass(p, r):
                def step(g, s, n, m, k, prev, nxt):
                    u = s % 2
                    a = group_tick(r, g)
                    if nxt:
                        transposed(1 - u, k, True)
                    if prev:
                        sums_out(1 - u, m)
                    act.wait_ge(s_sub, a)
                    act.nop(nofuse=True)
                    nc.scalar.activation(wt[:, u, :], sm[:, :], ACT.Exp).then_inc(wt_ready[u], 1)
                    act.wait_ge(s_diff, a)
                    act.nop(nofuse=True)
                    nc.scalar.activation(ed[:, u, :, :], diff[:, :, :], ACT.Exp).then_inc(s_ed, 1)

                transposed(0, ticks(p, 0, 0), True)
                pipeline(act, p, step, lambda g, s, n: sums_out(s % 2, n))

            with act.Fori(0, R) as r:
                attention_pass(LAYERS * R + r, r)

            with act.Fori(0, CB) as b:
                n = b + 1
                for u in range(2):
                    act.wait_ge(n_lin[u], CB + n)
                    act.nop(nofuse=True)
                    nc.scalar.activation(t2[:, u, :], bank[u][:, 0:CH], ACT.Identity, bias=col(BV)).then_inc(n_linc[u], 1)
                for u in range(2):
                    act.wait_ge(f_l[u], n)
                    act.nop(nofuse=True)
                    nc.scalar.activation(t3[:, u, :], bank[2 + u][:, 0:CH], ACT.Relu, bias=col(BL)).then_inc(f_o[u], 1)
                norm(CB + n)
                for u in range(2):
                    act.wait_ge(f_t[u], n)
                    act.nop(nofuse=True)
                    act.wait_ge(out_sem[u], n * 64)
                    act.nop(nofuse=True)
                    nc.scalar.copy(outn[:, u, :, :], bank[4 + u][0:PIECE, :].rearrange("p (k d) -> p k d", k=4)
                                   ).then_inc(f_n[u], 1)

        @block.vector
        def _(v):
            v_ = nc.vector
            v_.memset(xN[:, FULL:NT, :], 0.0).then_inc(const_done, 1)
            v_.memset(ones16[:, :], 1.0)
            v_.memset(inv_d[:, :], 1.0 / D)
            v_.memset(eps_c[:, :], EPS)
            v_.memset(relu[:, :, :, D:D + 1], 1.0).then_inc(const_done, 1)
            for s in (added[0] + added[1], res_done):
                for one in s:
                    v.sem_inc(one, 1)
            for u in range(2):
                v.sem_inc(summed[u], SLOTS // 2)
            v.wait_ge(loaded, 16 * LOADS)
            v.nop(nofuse=True)
            v_.tensor_reduce(rmin[:, :], rowsI[:, :], AX.X, ALU.min).then_inc(setup_dve, 1)
            v_.tensor_reduce(rmax[:, :], rowsI[:, :], AX.X, ALU.max).then_inc(setup_dve, 1)
            v.wait_ge(setup_dve, 2)
            v.nop(nofuse=True)
            v_.tensor_tensor(span[:, :], rmax[:, :], rmin[:, :], ALU.subtract).then_inc(setup_dve, 1)
            v.wait_ge(setup_pe, 1)
            v.nop(nofuse=True)
            v_.tensor_copy(base0[:, :], bank[2][0:1, 0:NG])
            v_.tensor_reduce(spanm[:, :], bank[2][0:1, NG:2 * NG], AX.X, ALU.max).then_inc(setup_dve, 1)
            v_.tensor_tensor(dst0[:, :].rearrange("p (g t) -> p g t", t=TG),
                             dstI[:, :].rearrange("p (g t) -> p g t", t=TG),
                             bank[2][:, 2 * NG:3 * NG].unsqueeze(2).to_broadcast([P, NG, TG]), ALU.subtract)
            v.wait_ge(setup_dve, 4)
            v.nop(nofuse=True)
            v.wait_ge(ident_done, 4)
            v.nop(nofuse=True)
            v_.tensor_copy(ident16[:, :], ident[:, :])
            v_.tensor_copy(iota16[:, :], iota_w[:, :, :].rearrange("p k n -> p (k n)"))
            v_.tensor_scalar(within[:, :], steps[:, :], spanm[:, :], None, ALU.is_le).then_inc(setup_dve, 1)
            v.wait_ge(setup_dve, 5)
            v.nop(nofuse=True)
            v_.reduce_sum(count[:, :], within[:, :], AX.X).then_inc(setup_dve, 1)
            v.wait_ge(setup_dve, 6)
            v.nop(nofuse=True)
            v_.tensor_copy(roundsI[:, :], count[:, :]).then_inc(ready_all, 1)
            v.wait_ge(setup_pe, 2)
            v.nop(nofuse=True)
            v_.tensor_copy(WkTb[:, 0:D], bank[3][:, P:2 * P])
            v_.tensor_copy(col(B2U), bank[3][:, 1:2])
            v_.tensor_copy(msgW2T[:, :], bank[3][:, 2 * P:3 * P]).then_inc(setup_dve, 1)
            b1_all, b1_res, (b1_hi, b1_mid, b1_lo) = tabA[:, 0, :], res[:, 0, :], (tabB[:, 0, k, :] for k in range(3))
            v_.tensor_copy(b1_hi, b1_all).then_inc(setup_dve, 1)
            v.wait_ge(setup_dve, 8)
            v.nop(nofuse=True)
            v_.tensor_scalar(b1parts[:, :], b1_hi, ident[:, 0:1], None, ALU.mult)
            v_.tensor_tensor(b1_res, b1_all, b1_hi, ALU.subtract).then_inc(setup_dve, 1)
            v.wait_ge(setup_dve, 9)
            v.nop(nofuse=True)
            v_.tensor_copy(b1_mid, b1_res).then_inc(setup_dve, 1)
            v.wait_ge(setup_dve, 10)
            v.nop(nofuse=True)
            v_.scalar_tensor_tensor(out=b1parts[:, :], in0=b1_mid, scalar=ident[:, 1:2], in1=b1parts[:, :],
                                    op0=ALU.mult, op1=ALU.add)
            v_.tensor_tensor(b1_lo, b1_res, b1_mid, ALU.subtract).then_inc(setup_dve, 1)
            v.wait_ge(setup_dve, 11)
            v.nop(nofuse=True)
            v_.scalar_tensor_tensor(out=b1parts[:, :], in0=b1_lo, scalar=ident[:, 2:3], in1=b1parts[:, :],
                                    op0=ALU.mult, op1=ALU.add).then_inc(setup_dve, 1)
            for k, first in enumerate(GROUPS4):
                m = min(4, NT - first)
                v.wait_ge(xt_done, k + 1)
                v.nop(nofuse=True)
                v_.tensor_copy(hT[:, first * P:(first + m) * P], xT[:, first * P:(first + m) * P])
            v_.reduce_sum(col(SUMX), xT[:, 0:N], AX.X).then_inc(setup_dve, 1)
            v.wait_ge(setup_dve, 13)
            v.nop(nofuse=True)
            v_.tensor_scalar(col(SUMX), col(SUMX), 1.0 / N, None, ALU.mult).then_inc(setup_dve, 1)
            v.wait_ge(setup_act, 1)
            v.nop(nofuse=True)
            v_.tensor_copy(msg_upd[:, :], bank[3][:, 3 * P:4 * P]).then_inc(u_h[0], 1)
            v_.tensor_tensor(gcol[:, :], col(GH), col(UB2), ALU.add).then_inc(u_h[1], 1)
            R = rounds(v)

            def split(q, width, b_at):
                with v.Fori(0, TB) as b:
                    n = q * TB + b + 1
                    for u in range(2):
                        v.wait_ge(hi_done[u], n)
                        v.nop(nofuse=True)
                        v_.tensor_tensor(res[:, u, 0:width], bank[u][:, b_at:b_at + width], tabB[:, u, 0, 0:width],
                                         ALU.subtract).then_inc(res_done[u], 1)
                        v.wait_ge(res_done[u], n + 1)
                        v.nop(nofuse=True)
                        v_.tensor_copy(tabB[:, u, 1, 0:width], res[:, u, 0:width]).then_inc(mid_done[u], 1)
                        v.wait_ge(mid_done[u], n)
                        v.nop(nofuse=True)
                        v_.tensor_tensor(tabB[:, u, 2, 0:width], res[:, u, 0:width], tabB[:, u, 1, 0:width],
                                         ALU.subtract).then_inc(lo_done[u], 1)

            def write_base():
                v_.tensor_scalar(baseI[:, :], baseF[:, :], float(NPAD - WIN), None, ALU.min).then_inc(base_ready, 1)

            def all_rounds(l, one_pass):
                t0 = l * (2 * R + 1)
                v_.tensor_copy(baseF[:, :], base0[:, :])
                v_.tensor_copy(dst_rel[:, :], dst0[:, :]).then_inc(moved, 1)
                v.wait_ge(moved, t0 + 1)
                v.nop(nofuse=True)
                with v.Fori(0, R) as r:
                    v_.tensor_copy(rel16[:, :], dst_rel[:, :]).then_inc(moved, 1)
                    write_base()
                    v.wait_ge(moved, t0 + 2 * r + 2)
                    v.nop(nofuse=True)
                    one_pass(r)
                    v_.tensor_scalar(baseF[:, :], baseF[:, :], float(WIN), None, ALU.add)
                    v_.tensor_scalar(dst_rel[:, :], dst_rel[:, :], float(-WIN), None, ALU.add).then_inc(moved, 1)
                    v.wait_ge(moved, t0 + 2 * r + 3)
                    v.nop(nofuse=True)

            def one_hot(g, u):
                rel = rel16[:, bass.ds(g * TG, TG)].unsqueeze(2).to_broadcast([P, TG, 3 * WIN])
                nodes = iota16[:, :].unsqueeze(1).to_broadcast([P, TG, 3 * WIN])
                v_.tensor_tensor(oh[:, u, :, :], nodes, rel,
                                 ALU.is_equal).then_inc(oh_ready[u], 1)

            def weigh(u, n):
                v.wait_ge(wt_ready[u], n)
                v.nop(nofuse=True)
                v_.tensor_tensor(ohw[:, u, :, :], oh[:, u, :, 0:WIN],
                                 wt[:, u, :].unsqueeze(2).to_broadcast([P, TG, WIN]), ALU.mult
                                 ).then_inc(ohw_ready[u], 1)

            def message_pass(p):
                def add(u, n, q):
                    v.wait_ge(picked[u][q], n)
                    v.nop(nofuse=True)
                    v.wait_ge(gathered[u][q], n * 32)
                    v.nop(nofuse=True)
                    v_.tensor_tensor(pre[:, u, 2 * q:2 * q + 2, :], arow[:, u, 2 * q:2 * q + 2, :], bg[q],
                                     ALU.add).then_inc(added[u][q], 1)

                def dot(u, n, q):
                    v.wait_ge(added[u][q], n + 1)
                    v.nop(nofuse=True)
                    for t in (2 * q, 2 * q + 1):
                        ins = v_.scalar_tensor_tensor(out=junk[:, t, 0:D], in0=pre[:, u, t, D:2 * D], scalar=0.0,
                                                      in1=attw[:, :], op0=ALU.max, op1=ALU.mult,
                                                      accum_out=lg[:, u, t:t + 1])
                    ins.then_inc(dotted[u][q], 1)

                def merge(row, u, n):
                    v.wait_ge(scat_done[u], n)
                    v.nop(nofuse=True)
                    at = acc[:, :, bass.ds(row, WIN)]
                    v_.tensor_tensor(at, at, sc_sum[u], ALU.add).then_inc(merged[u], 1)

                def step(g, s, n, m, k, prev, nxt):
                    u = s % 2
                    add(u, n, 0)
                    add(u, n, 1)
                    dot(u, n, 0)
                    add(u, n, 2)
                    add(u, n, 3)
                    if nxt:
                        if prev:
                            v.wait_ge(ohw_ready[1 - u], m)
                            v.nop(nofuse=True)
                        one_hot(g + 1, 1 - u)
                    dot(u, n, 1)
                    dot(u, n, 2)
                    dot(u, n, 3)
                    if prev:
                        merge(window(v, g - 1), 1 - u, m)
                    weigh(u, n)

                v.wait_ge(base_ready, p + 1)
                v.nop(nofuse=True)
                one_hot(0, 0)
                pipeline(v, p, step, lambda g, s, n: merge(window(v, g), s % 2, n))

            def update(l):
                with v.Fori(0, CB) as b:
                    n = l * CB + b + 1
                    for u in range(2):
                        v.wait_ge(u_lin[u], n)
                        v.nop(nofuse=True)
                        v_.scalar_tensor_tensor(out=t1[:, u, :], in0=acc[:, 1, bass.ds((2 * b + u) * CH, CH)],
                                                scalar=col(B2U), in1=bank[u][:, 0:CH], op0=ALU.mult, op1=ALU.add
                                                ).then_inc(u_pre[u], 1)
                    for u in range(2):
                        v.wait_ge(u_new[u], n)
                        v.nop(nofuse=True)
                        h = chunk(hT, 2 * b + u)
                        v_.scalar_tensor_tensor(out=h, in0=bank[4 + u][:, 0:CH], scalar=gcol[:, :], in1=h,
                                                op0=ALU.add, op1=ALU.add).then_inc(u_h[u], 1)

            with v.Fori(0, LAYERS) as l:
                split(l, 2 * D, 2 * D)
                v.wait_ge(acc_zero, l + 1)
                v.nop(nofuse=True)
                all_rounds(l, lambda r: message_pass(l * R + r))
                update(l)

            def norm(q, b, into):
                for u in range(2):
                    v.wait_ge(n_mu[u], q)
                    v.nop(nofuse=True)
                    v_.tensor_tensor(t2[:, u, :], t1[:, u, :], bank[u][:, 0:CH], ALU.subtract).then_inc(n_d[u], 1)
                for u in range(2):
                    v.wait_ge(n_std[u], q)
                    v.nop(nofuse=True)
                    v_.reciprocal(t1[:, u, :], t3[:, u, :]).then_inc(n_r[u], 1)
                for u in range(2):
                    v.wait_ge(n_r[u], q)
                    v.nop(nofuse=True)
                    v_.tensor_tensor(into(u), t2[:, u, :], t1[:, u, :], ALU.mult).then_inc(n_x1[u], 1)
                v.wait_ge(n_x1[1], q)
                v.nop(nofuse=True)

            v.wait_ge(u_h[1], LAYERS * CB + 1)
            v.nop(nofuse=True)
            with v.Fori(0, CB) as b:
                for u in range(2):
                    v_.tensor_tensor(t1[:, u, :], chunk(hT, 2 * b + u), chunk(xT, 2 * b + u), ALU.add
                                     ).then_inc(n_y[u], 1)
                norm(b + 1, b, lambda u: chunk(hT, 2 * b + u))
            split(LAYERS, D + 1, D)

            def attention_pass(p, r):
                def dot(s, n, q):
                    u = s % 2
                    v.wait_ge(picked[u][q], n)
                    v.nop(nofuse=True)
                    v.wait_ge(gathered[u][q], n * 32)
                    v.nop(nofuse=True)
                    for t in (2 * q, 2 * q + 1):
                        at = (t % 2) * 2 * D
                        ins = v_.scalar_tensor_tensor(out=junk[:, t, :], in0=bank[q % 2][:, at:at + D + 1], scalar=1.0,
                                                      in1=xrow[:, s, t, :], op0=ALU.mult, op1=ALU.mult,
                                                      accum_out=lg[:, u, t:t + 1])
                    ins.then_inc(dotted[u][q], 1)

                def node_max(u, n, a):
                    v.wait_ge(mask_ready, a)
                    v.nop(nofuse=True)
                    v.wait_ge(s_spread, a)
                    v.nop(nofuse=True)
                    v_.tensor_tensor_reduce(out=junkm[:, :], in0=score_ps, in1=mask[:, u, :], scale=1.0,
                                            scalar=-BIG / 2, op0=ALU.add, op1=ALU.max, accum_out=mloc[:, :]
                                            ).then_inc(s_max, 1)
                    v.wait_ge(s_max, a)
                    v.nop(nofuse=True)
                    v_.tensor_copy(m3[:, 0:1], mloc[:, :]).then_inc(s_hi, 1)
                    v.wait_ge(s_hi, a)
                    v.nop(nofuse=True)
                    v_.tensor_tensor(m3[:, 1:2], mloc[:, :], m3[:, 0:1], ALU.subtract)
                    v_.tensor_tensor(mres[:, :], mloc[:, :], m3[:, 0:1], ALU.subtract).then_inc(s_mid, 1)
                    v.wait_ge(s_mid, a)
                    v.nop(nofuse=True)
                    v_.tensor_tensor(m3[:, 2:3], mres[:, :], m3[:, 1:2], ALU.subtract).then_inc(s_lo, 1)

                def less_max(u, a):
                    v.wait_ge(s_me, a)
                    v.nop(nofuse=True)
                    v_.tensor_reduce(me[:, :], sc_me, AX.X, ALU.add).then_inc(s_mer, 1)
                    v.wait_ge(s_mer, a)
                    v.nop(nofuse=True)
                    v_.tensor_tensor(sm[:, :], lg[:, u, :], me[:, :], ALU.subtract).then_inc(s_sub, 1)

                def merge_max(row, a, prev):
                    old = mrun[:, bass.ds(row, WIN)]
                    v_.tensor_tensor(mnew[:, :], sc_max, old, ALU.max).then_inc(s_mnew, 1)
                    v.wait_ge(s_mnew, a)
                    v.nop(nofuse=True)
                    if prev:
                        v.wait_ge(s_ed, a - 1)
                        v.nop(nofuse=True)
                    v_.tensor_tensor(diff[:, 0, :], old, mnew[:, :], ALU.subtract)
                    v_.tensor_tensor(diff[:, 1, :], sc_max, mnew[:, :], ALU.subtract).then_inc(s_diff, 1)

                def merge(row, u, n, a):
                    at = acc[:, :, bass.ds(row, WIN)]
                    v.wait_ge(s_ed, a)
                    v.nop(nofuse=True)
                    v.wait_ge(scat_done[u], n)
                    v.nop(nofuse=True)
                    v_.tensor_tensor(newsc[:, :, :], sc_sum[u], ed[:, u, 1:2, :].to_broadcast([P, 2, WIN]), ALU.mult)
                    v_.tensor_tensor(oldsc[:, :, :], at, ed[:, u, 0:1, :].to_broadcast([P, 2, WIN]), ALU.mult
                                     ).then_inc(s_scaled, 1)
                    v.wait_ge(s_scaled, a)
                    v.nop(nofuse=True)
                    v_.tensor_tensor(at, newsc[:, :, :], oldsc[:, :, :], ALU.add).then_inc(merged[u], 1)

                def step(g, s, n, m, k, prev, nxt):
                    u = s % 2
                    a = group_tick(r, g)
                    dot(s, n, 0)
                    dot(s, n, 1)
                    if nxt:
                        if prev:
                            v.wait_ge(ohw_ready[1 - u], m)
                            v.nop(nofuse=True)
                        one_hot(g + 1, 1 - u)
                    dot(s, n, 2)
                    dot(s, n, 3)
                    if prev:
                        row_before = window(v, g - 1)
                    node_max(u, n, a)
                    row = window(v, g)
                    less_max(u, a)
                    merge_max(row, a, prev)
                    weigh(u, n)
                    v.wait_ge(s_diff, a)
                    v.nop(nofuse=True)
                    v_.tensor_copy(mrun[:, bass.ds(row, WIN)], mnew[:, :])
                    if prev:
                        merge(row_before, 1 - u, m, a - 1)

                def tail(g, s, n):
                    v.wait_ge(merged[1 - s % 2], n)
                    v.nop(nofuse=True)
                    merge(window(v, g), s % 2, n, group_tick(r, g))

                v.wait_ge(base_ready, p + 1)
                v.nop(nofuse=True)
                one_hot(0, 0)
                pipeline(v, p, step, tail)

            v.wait_ge(acc_zero, LAYERS + 3)
            v.nop(nofuse=True)
            all_rounds(LAYERS, lambda r: attention_pass(LAYERS * R + r, r))

            v.wait_ge(merged[1], (LAYERS + 1) * (R * BODIES))
            v.nop(nofuse=True)
            with v.Fori(0, CB) as b:
                n = b + 1
                for u in range(2):
                    v_.tensor_scalar(t1[:, u, :], acc[:, 1, bass.ds((2 * b + u) * CH, CH)], 1e-30, None, ALU.max
                                     ).then_inc(f_inv[u], 1)
                for u in range(2):
                    v.wait_ge(f_inv[u], 2 * b + 1)
                    v.nop(nofuse=True)
                    v_.reciprocal(t2[:, u, :], t1[:, u, :]).then_inc(f_inv[u], 1)
                for u in range(2):
                    v_.scalar_tensor_tensor(out=aggs[:, u, :], in0=acc[:, 1, bass.ds((2 * b + u) * CH, CH)], scalar=0.0,
                                            in1=chunk(hT, 2 * b + u), op0=ALU.is_le, op1=ALU.mult)
                for u in range(2):
                    v.wait_ge(f_inv[u], 2 * b + 2)
                    v.nop(nofuse=True)
                    v_.tensor_tensor(t1[:, u, :], acc[:, 0, bass.ds((2 * b + u) * CH, CH)], t2[:, u, :], ALU.mult
                                     ).then_inc(f_avg[u], 1)
                for u in range(2):
                    v.wait_ge(f_avg[u], n)
                    v.nop(nofuse=True)
                    v_.tensor_tensor(t1[:, u, :], t1[:, u, :], aggs[:, u, :], ALU.add).then_inc(f_sel[u], 1)
                for u in range(2):
                    v.wait_ge(f_o[u], n)
                    v.nop(nofuse=True)
                    v_.tensor_tensor(t1[:, u, :], t3[:, u, :], chunk(hT, 2 * b + u), ALU.add).then_inc(n_y[u], 1)
                norm(CB + n, b, lambda u: t3[:, u, :])

        @block.tensor
        def _(pe):
            mm, tr = nc.tensor.matmul, nc.tensor.transpose
            pe.wait_ge(loaded, 16 * LOADS)
            pe.nop(nofuse=True)
            pe.wait_ge(ident_done, 4)
            pe.nop(nofuse=True)
            pe.wait_ge(const_done, 2)
            pe.nop(nofuse=True)
            pe.wait_ge(setup_dve, 3)
            pe.nop(nofuse=True)
            mm(bank[2][0:1, 0:NG], rmin[:, :], ident[0:NG, 0:NG], start=True, stop=True)
            mm(bank[2][0:1, NG:2 * NG], span[:, :], ident[0:NG, 0:NG], start=True, stop=True)
            mm(bank[2][:, 2 * NG:3 * NG], rmin[:, 0:1].to_broadcast([NG, P]), ident[0:NG, 0:NG],
               start=True, stop=True).then_inc(setup_pe, 1)
            tr(bank[3][:, P:2 * P], Wk[:, :], ident[:, :])
            mm(bank[3][:, 1:2], updW1[:, 1, :], col(B2), start=True, stop=True)
            tr(bank[3][:, 2 * P:3 * P], msgW2[:, :], ident[:, :]).then_inc(setup_pe, 1)
            pe.wait_ge(loaded_tail, 16)
            pe.nop(nofuse=True)
            for k, first in enumerate(GROUPS4):
                if k >= 2:
                    pe.wait_ge(xt_done, k - 1)
                    pe.nop(nofuse=True)
                for t in range(first, min(first + 4, NT)):
                    ins = tr(bank[k % 2][:, (t - first) * P:(t - first + 1) * P], xN[:, t, :], ident[:, :])
                ins.then_inc(xt_ps, 1)
            pe.wait_ge(setup_dve, 14)
            pe.nop(nofuse=True)
            mm(bank[3][:, 3 * P:4 * P], msgW2T[:, :], updW1[:, 1, :], start=True, stop=True)
            mm(bank[3][:, 0:1], glbW[:, :], col(SUMX), start=True, stop=True).then_inc(setup_pe, 1)
            R = rounds(pe)

            def tables(q, product):
                with pe.Fori(0, TB) as b:
                    n = q * TB + b + 1
                    for u in range(2):
                        pe.wait_ge(staged[u], n)
                        pe.nop(nofuse=True)
                        pe.wait_ge(res_done[u], n)
                        pe.nop(nofuse=True)
                        product(u).then_inc(tab_ps[u], 1)

            def message_rows(u):
                mm(bank[u], stage[:, u, 0, :], wcat[:, :], start=True, stop=False)
                return mm(bank[u][:, 2 * D:4 * D], ones16[:, :], b1parts[:, :], start=False, stop=True)

            def attention_rows(u):
                tr(bank[u][:, 0:D], stage[:, u, 0, :], ident[:, :])
                return mm(bank[u][:, D:2 * D + 1], stage[:, u, 1, :], WkTb[:, :], start=True, stop=True)

            def turn(u, n):
                pe.wait_ge(oh_ready[u], n)
                pe.nop(nofuse=True)
                for t in range(TG):
                    ins = tr(ohp[u][0:3 * WIN, t * P:(t + 1) * P], oh[:, u, t, :], ident16[:, :])
                ins.then_inc(ohp_ready[u], 1)

            def pick(u, q, into, win, width):
                for t in (2 * q, 2 * q + 1):
                    at = (t % 2) * 2 * D
                    ins = mm(into[:, at:at + width], oht[:, u, t * P:(t + 1) * P], win[:, u, :], start=True, stop=True)
                return ins

            def scatter(u, n, rows, part):
                if part[0] == 0:
                    pe.wait_ge(ohw_ready[u], n)
                    pe.nop(nofuse=True)
                for t in part:
                    ins = mm(scat[u][0:WIN, 0:D + 1], ohw[:, u, t, :], rows[:, t, :], start=(t == 0), stop=(t == TG - 1))
                if part[-1] == TG - 1:
                    ins.then_inc(summed[u], 1)

            def turn_sums(u, n):
                pe.wait_ge(sum_out[u], n)
                pe.nop(nofuse=True)
                tr(sc_sum[u][:, 0, :], ssum[:, u, 0:D], ident[0:WIN, 0:WIN])
                tr(sc_sum[u][:, 1, :], ssum[:, u, D:D + 1].to_broadcast([WIN, P]), ident[0:WIN, 0:WIN]
                   ).then_inc(scat_done[u], 1)

            def message_pass(p):
                def rows(u, n, m, q):
                    if q == 0:
                        pe.wait_ge(win_ld[u], n * 48)
                        pe.nop(nofuse=True)
                    pe.wait_ge(oht_ready[u][q // 2], n)
                    pe.nop(nofuse=True)
                    pe.wait_ge(added[1 - u][q], m + 1)
                    pe.nop(nofuse=True)
                    pick(u, q, bank[q], bwin, 2 * D).then_inc(picked[u][q], 1)

                def step(g, s, n, m, k, prev, nxt):
                    u = s % 2
                    before = relu[:, 1 - u, :, :]
                    for q in range(PAIRS):
                        rows(u, n, m, q)
                    if prev:
                        scatter(1 - u, m, before, range(TG))
                        turn_sums(1 - u, m)
                    if nxt:
                        turn(1 - u, k)

                def tail(g, s, n):
                    scatter(s % 2, n, relu[:, s % 2, :, :], range(TG))
                    turn_sums(s % 2, n)

                turn(0, ticks(p, 0, 0))
                pipeline(pe, p, step, tail)

            def update(l):
                pe.wait_ge(merged[1], (l + 1) * (R * BODIES))
                pe.nop(nofuse=True)
                with pe.Fori(0, CB) as b:
                    n = l * CB + b + 1
                    for u in range(2):
                        at = bass.ds((2 * b + u) * CH, CH)
                        mm(bank[u][:, 0:CH], updW1[:, 0, :], hT[:, at], start=True, stop=False)
                        mm(bank[u][:, 0:CH], msg_upd[:, :], acc[:, 0, at], start=False, stop=True).then_inc(u_lin[u], 1)
                    for u in range(2):
                        pe.wait_ge(u_relu[u], n)
                        pe.nop(nofuse=True)
                        pe.wait_ge(u_h[u], n)
                        pe.nop(nofuse=True)
                        mm(bank[4 + u][:, 0:CH], updW2[:, :], hid[:, u, :], start=True, stop=True
                           ).then_inc(u_new[u], 1)

            with pe.Fori(0, LAYERS) as l:
                tables(l, message_rows)
                with pe.Fori(0, R) as r:
                    message_pass(l * R + r)
                update(l)

            def norm(q):
                for u in range(2):
                    pe.wait_ge(n_y[u], q)
                    pe.nop(nofuse=True)
                    mm(bank[u][:, 0:CH], inv_d[:, :], t1[:, u, :], start=True, stop=True).then_inc(n_mu[u], 1)
                for u in range(2):
                    pe.wait_ge(n_sq[u], q)
                    pe.nop(nofuse=True)
                    mm(bank[2 + u][:, 0:CH], inv_d[:, :], t3[:, u, :], start=True, stop=True).then_inc(n_var[u], 1)

            with pe.Fori(0, CB) as b:
                norm(b + 1)
                for u in range(2):
                    pe.wait_ge(n_x1[u], b + 1)
                    pe.nop(nofuse=True)
                    mm(bank[4 + u][:, 0:CH], Wq[:, :], chunk(hT, 2 * b + u), start=True, stop=True
                       ).then_inc(n_lin[u], 1)
            tables(LAYERS, attention_rows)

            def attention_pass(p, r):
                def rows(u, n, q):
                    if q == 0:
                        pe.wait_ge(win_ld[u], n * 48)
                        pe.nop(nofuse=True)
                    if q >= 2:
                        pe.wait_ge(dotted[u][q - 2], n)
                        pe.nop(nofuse=True)
                    pe.wait_ge(oht_ready[u][q // 2], n)
                    pe.nop(nofuse=True)
                    pick(u, q, bank[q % 2], qwin, D + 1).then_inc(picked[u][q], 1)

                def spread(u, n, q):
                    pe.wait_ge(dotted[u][q], n)
                    pe.nop(nofuse=True)
                    for t in (2 * q, 2 * q + 1):
                        ins = tr(score_ps[:, t * P:(t + 1) * P], lg[:, u, t:t + 1].to_broadcast([P, WIN]), ident[:, :])
                    return ins

                def step(g, s, n, m, k, prev, nxt):
                    u = s % 2
                    a = group_tick(r, g)
                    before = xrow[:, (s - 1) % SLOTS, :, :]
                    rows(u, n, 0)
                    rows(u, n, 1)
                    if prev:
                        scatter(1 - u, m, before, range(0, 4))
                    spread(u, n, 0)
                    rows(u, n, 2)
                    spread(u, n, 1)
                    rows(u, n, 3)
                    spread(u, n, 2)
                    spread(u, n, 3).then_inc(s_spread, 1)
                    if nxt:
                        turn(1 - u, k)
                    if prev:
                        scatter(1 - u, m, before, range(4, 8))
                    pe.wait_ge(s_lo, a)
                    pe.nop(nofuse=True)
                    for t in range(TG):
                        mm(sc_me[:, t, :], oht[0:WIN, u, t * P:(t + 1) * P], m3[:, :], start=True, stop=True)
                    tr(sc_max, mloc[:, 0:1].to_broadcast([WIN, P]), ident[0:WIN, 0:WIN]).then_inc(s_me, 1)
                    if prev:
                        turn_sums(1 - u, m)

                def tail(g, s, n):
                    scatter(s % 2, n, xrow[:, s, :, :], range(TG))
                    turn_sums(s % 2, n)

                turn(0, ticks(p, 0, 0))
                pipeline(pe, p, step, tail)

            with pe.Fori(0, R) as r:
                attention_pass(LAYERS * R + r, r)

            with pe.Fori(0, CB) as b:
                n = b + 1
                for u in range(2):
                    pe.wait_ge(f_sel[u], n)
                    pe.nop(nofuse=True)
                    mm(bank[u][:, 0:CH], Wv[:, :], t1[:, u, :], start=True, stop=True).then_inc(n_lin[u], 1)
                for u in range(2):
                    pe.wait_ge(n_linc[u], CB + n)
                    pe.nop(nofuse=True)
                    mm(bank[2 + u][:, 0:CH], Wl[:, :], t2[:, u, :], start=True, stop=True).then_inc(f_l[u], 1)
                norm(CB + n)
                for u in range(2):
                    pe.wait_ge(n_x1[u], CB + n)
                    pe.nop(nofuse=True)
                    for k in range(4):
                        ins = tr(bank[4 + u][0:PIECE, k * D:(k + 1) * D], t3[:, u, k * PIECE:(k + 1) * PIECE],
                                 ident[:, :])
                    ins.then_inc(f_t[u], 1)


_GNN = ("msg_W1", "msg_b1", "msg_W2", "msg_b2", "upd_W1", "upd_b1", "upd_W2", "upd_b2",
        "att_W1", "att_b1", "att_W2", "att_b2", "glb_W", "glb_b")
_ATT = ("Wq", "bq", "Wk", "bk", "Wv", "bv", "Wl", "bl")


def kernel(**inputs):
    import concourse.bacc as bacc
    from concourse.bass_utils import run_bass_kernel_spmd

    def padded(name, fill):
        a = np.full((NG * TG * P,), fill, np.int32)
        a[:E] = np.asarray(inputs[name])
        return a.reshape(NG, TG, P)

    src, dst = padded("src", 0), padded("dst", N)
    arrays = {
        "x": np.ascontiguousarray(inputs["x"]),
        "idx": np.ascontiguousarray(src.transpose(0, 2, 1)).reshape(NG * P, TG),
        "dst_pm": np.ascontiguousarray(dst.transpose(2, 0, 1)).reshape(P, NG * TG),
        "dst_gm": dst.reshape(NG, TG * P),
    }
    for prefix, names in (("L0_gnn_", _GNN), ("L1_gnn_", _ATT)):
        for n in names:
            arrays[n] = np.ascontiguousarray(inputs[prefix + n])
    nc = bacc.Bacc("TRN2", target_bir_lowering=False, num_devices=1)
    aps = {n: nc.dram_tensor(f"in_{n}", a.shape, mybir.dt.from_np(a.dtype), kind="ExternalInput").ap()
           for n, a in arrays.items()}
    out = nc.dram_tensor("out_0", (N, D), F32, kind="ExternalOutput").ap()
    build(nc, aps["x"], aps["idx"], aps["dst_pm"], aps["dst_gm"], aps, out)
    r = run_bass_kernel_spmd(nc, [{f"in_{n}": a for n, a in arrays.items()}], core_ids=[0])
    return r.results[0]["out_0"]
```

```python
import concourse.bass as bass
import concourse.mybir as mybir
import numpy as np
from contextlib import ExitStack

F32, BF16, I32 = mybir.dt.float32, mybir.dt.bfloat16, mybir.dt.int32
ALU, ACT, AX = mybir.AluOpType, mybir.ActivationFunctionType, mybir.AxisListType

P = 128
N, E, D = 3125, 100000, 128
NT = 26
NPAD = NT * P
CH = NPAD // 8
TG = 8
NG = 98
BODIES = NG // 2
WIN = 42
PAIRS = TG // 2
LAYERS = 2
SLOTS = 4
ROUNDS = -(-(N + 1) // WIN)
BIG = 3.0e38
PIECE = CH // 4
EPS = 1e-5


def build(nc, x, idx, dst_pm, dst_gm, w, out):
    A_tab = nc.dram_tensor("A_tab", (NPAD, 2 * D), F32, kind="Internal").ap()
    B_tab = nc.dram_tensor("B_tab", (NPAD, 3 * 2 * D), BF16, kind="Internal").ap()
    X_tab = nc.dram_tensor("X_tab", (NPAD, D), F32, kind="Internal").ap()
    Q_tab = nc.dram_tensor("Q_tab", (NPAD, 3 * (D + 1)), BF16, kind="Internal").ap()

    with ExitStack() as ctx:
        def sb(name, shape, dt=F32):
            return ctx.enter_context(nc.sbuf_tensor(name, shape, dt))

        def pb(name, shape, dt=F32):
            return ctx.enter_context(nc.psum_tensor(name, shape, dt))

        def sem(name):
            return ctx.enter_context(nc.semaphore(name))

        def sems(name, *dims):
            if not dims:
                return sem(name)
            return [sems(f"{name}_{k}", *dims[1:]) for k in range(dims[0])]

        hT = sb("hT", [P, NPAD])
        xT = sb("xT", [P, NPAD])
        xN = sb("xN", [P, NT, D])
        acc = sb("acc", [P, 2, NPAD])
        mrun = sb("mrun", [P, NPAD])
        ident = sb("ident", [P, P])
        iota_w = sb("iota_w", [P, 3, WIN])
        ident16 = sb("ident16", [P, P], BF16)
        iota16 = sb("iota16", [P, 3 * WIN], BF16)
        rel16 = sb("rel16", [P, NG * TG], BF16)
        centre = sb("centre", [P, P])
        unused = sb("unused", [P, 1])
        eps_c = sb("eps_c", [P, 1])
        dstI = sb("dstI", [P, NG * TG], I32)
        dst0 = sb("dst0", [P, NG * TG])
        dst_rel = sb("dst_rel", [P, NG * TG])
        rowsI = sb("rowsI", [NG, TG * P], I32)
        rmin = sb("rmin", [NG, 1])
        rmax = sb("rmax", [NG, 1])
        span = sb("span", [NG, 1])
        base0 = sb("base0", [1, NG])
        baseF = sb("baseF", [1, NG])
        baseI = sb("baseI", [1, NG], I32)
        spanm = sb("spanm", [1, 1])
        steps = sb("steps", [1, ROUNDS])
        within = sb("within", [1, ROUNDS])
        count = sb("count", [1, 1])
        roundsI = sb("roundsI", [1, 1], I32)
        wcat = sb("wcat", [P, 4 * D])
        b1parts = sb("b1parts", [P, 2 * D], BF16)
        ones16 = sb("ones16", [P, P], BF16)
        attw = sb("attw", [P, D])
        attb = sb("attb", [P, 1])
        msgW2 = sb("msgW2", [P, D])
        msgW2T = sb("msgW2T", [P, D])
        msg_upd = sb("msg_upd", [P, D])
        updW1 = sb("updW1", [P, 2, D])
        updW2 = sb("updW2", [P, D])
        glbW = sb("glbW", [P, D])
        Wq = sb("Wq", [P, D])
        Wk = sb("Wk", [P, D])
        WqT = sb("WqT", [P, D])
        WvT = sb("WvT", [P, D])
        Wqk = sb("Wqk", [P, D + 1])
        qk_parts = sb("qk_parts", [P, D + 1], BF16)
        Wvl = sb("Wvl", [P, D])
        bvl = sb("bvl", [P, D])
        WkTb = sb("WkTb", [P, D + 1])
        Wv = sb("Wv", [P, D])
        Wl = sb("Wl", [P, D])
        cols = sb("cols", [P, 9])
        UB1, UB2, GLB, BQ, BV, SUMX, GH, B2, B2U = range(9)
        gcol = sb("gcol", [P, 1])

        def col(k):
            return cols[:, k:k + 1]

        idx_st = sb("idx_st", [P, 2, TG], I32)
        rows_sb = sb("rows_sb", [P, SLOTS * TG * (D + 1)])
        arow = rows_sb[:, 0:2 * TG * 2 * D].rearrange("p (u t d) -> p u t d", u=2, t=TG)
        xrow = rows_sb[:, :].rearrange("p (s t d) -> p s t d", s=SLOTS, t=TG)
        bwin = sb("bwin", [3 * WIN, 2, 2 * D], BF16)
        qwin = sb("qwin", [3 * WIN, 2, D + 1], BF16)
        oh = sb("oh", [P, 2, TG, 3 * WIN], BF16)
        oht = sb("oht", [3 * WIN, 2, TG * P], BF16)
        mask = sb("mask", [WIN, 2, TG * P], BF16)
        pre = sb("pre", [P, 2, TG, 2 * D])
        ohw = sb("ohw", [P, 2, TG, WIN])
        relu = sb("relu", [P, 2, TG, D + 1])
        junk = sb("junk", [P, TG, D + 1], BF16)
        junkm = sb("junkm", [WIN, TG * P], BF16)
        lg = sb("lg", [P, 2, TG])
        wt = sb("wt", [P, 2, TG])
        sm = sb("sm", [P, TG])
        ssum = sb("ssum", [WIN, 2, D + 1])
        me = sb("me", [P, TG])
        mloc = sb("mloc", [WIN, 1])
        mres = sb("mres", [WIN, 1])
        m3 = sb("m3", [WIN, 3], BF16)
        mnew = sb("mnew", [P, WIN])
        diff = sb("diff", [P, 2, WIN])
        ed = sb("ed", [P, 2, 2, WIN])
        newsc = sb("newsc", [P, 2, WIN])
        oldsc = sb("oldsc", [P, 2, WIN])
        stage = sb("stage", [P, 2, P])
        tabA = sb("tabA", [P, 4, 2 * D])
        tabB = sb("tabB", [P, 4, 3, 2 * D], BF16)
        res = sb("res", [P, 2, 2 * D])
        hid = sb("hid", [P, 2, CH])
        t1 = sb("t1", [P, 2, CH])
        t2 = sb("t2", [P, 2, CH])
        yc, ysq, x1n = (xN[0:PIECE, 8 * k:8 * (k + 1), :].rearrange("p (u k) d -> p u k d", u=2) for k in range(3))
        outn = sb("outn", [PIECE, 2, 4, D])
        ysum, ymean, yvar, ystd, yinv, winv = (sb(n, [PIECE, 2, 4]) for n in (
            "ysum", "ymean", "yvar", "ystd", "yinv", "winv"))


        psum = pb("psum_main", [P, 6 * 512])
        bank = [psum[:, k * 512:(k + 1) * 512] for k in range(6)]
        scat = [pb(f"scat{k}", [P, 512]) for k in range(2)]
        bg = [bank[k].rearrange("p (t n) -> p t n", t=2) for k in range(4)]
        ohp = [bank[4 + u].bitcast(BF16) for u in range(2)]
        rows_ps = [bank[u][0:PIECE, :].rearrange("p (k d) -> p k d", k=4) for u in range(2)]
        score_ps = psum[0:WIN, 2 * 512:4 * 512]
        sc_sum = [scat[k][:, 256:256 + 2 * WIN].rearrange("p (a n) -> p a n", a=2) for k in range(2)]
        sc_max = bank[2][:, 0:WIN]
        sc_me = bank[2][:, WIN:WIN + 3 * TG].rearrange("p (t k) -> p t k", k=3)

        loaded, loaded_tail = sem("loaded"), sem("loaded_tail")
        const_done = sem("const_done")
        ident_done = sem("ident_done")
        setup_dve, setup_pe, setup_act = sem("setup_dve"), sem("setup_pe"), sem("setup_act")
        xt_ps, xt_done = sem("xt_ps"), sem("xt_done")
        ready_all = sem("ready_all")
        moved = sem("moved")
        base_ready = sem("base_ready")
        acc_zero = sem("acc_zero")
        staged, tab_ps, a_copied, hi_done, res_done, mid_done, lo_done = (sems(n, 2) for n in (
            "staged", "tab_ps", "a_copied", "hi_done", "res_done", "mid_done", "lo_done"))
        a_out, b_out = sems("a_out", 4), sems("b_out", 4)
        idx_ld, win_ld = sems("idx_ld", 2), sems("win_ld", 2)
        gathered = sems("gathered", 2, PAIRS)
        oh_ready, ohp_ready, oht_ready, mask_ready = sems("oh_ready", 2), sems("ohp_ready", 2), sems("oht_ready", 2, 2), sem("mask_ready")
        picked, dotted = sems("picked", 2, PAIRS), sems("dotted", 2, PAIRS)
        added = sems("added", 2, PAIRS)
        wt_ready, ohw_ready, summed, sum_out, scat_done, merged = (sems(n, 2) for n in (
            "wt_ready", "ohw_ready", "summed", "sum_out", "scat_done", "merged"))
        u_lin, u_pre, u_relu, u_new, u_h = (sems(n, 2) for n in ("u_lin", "u_pre", "u_relu", "u_new", "u_h"))
        n_y, n_rows, n_mu, n_d, n_c, n_var, n_std, n_r, n_x1, n_turned, n_back, x_out = (sems(n, 2) for n in (
            "n_y", "n_rows", "n_mu", "n_d", "n_c", "n_var", "n_std", "n_r", "n_x1", "n_turned", "n_back", "x_out"))
        (s_spread, s_max, s_hi, s_mid, s_lo, s_me, s_mer, s_sub, s_mnew, s_diff, s_ed, s_scaled) = (
            sem(n) for n in ("s_spread", "s_max", "s_hi", "s_mid", "s_lo", "s_me", "s_mer", "s_sub",
                             "s_mnew", "s_diff", "s_ed", "s_scaled"))
        f_kept, f_sel, f_rows, f_winv, f_mul, x1_ld = (sems(n, 2) for n in (
            "f_kept", "f_sel", "f_rows", "f_winv", "f_mul", "x1_ld"))
        out_sem = sems("out_sem", 2)

        block = ctx.enter_context(nc.Block())
        LOADS = 27
        FULL, REST = N // P, N % P
        TB = NT // 2
        TL = (TB - 1) // 2
        CB = NPAD // CH // 2
        GROUPS4 = list(range(0, NT, 4))

        def rounds(eng):
            eng.wait_ge(ready_all, 1)
            eng.nop(nofuse=True)
            return eng.value_load(roundsI[0:1, 0:1], min_val=1, max_val=ROUNDS)

        def window(eng, g):
            return eng.value_load(baseI[0:1, bass.ds(g, 1)], min_val=0, max_val=NPAD - WIN)

        def chunk(t, c):
            return t[:, bass.ds(c * CH, CH)]

        def uses(w):
            return TL + (w < 2)

        def table_loop(eng, q, part):
            def some(b, count):
                part([(4 * b + w, w, w % 2, q * TB + 2 * b + w // 2 + 1, q * uses(w) + b + 1) for w in range(count)])

            with eng.Fori(0, TL) as b:
                some(b, 4)
            some(TL, 2)

        def group_tick(r, g):
            return r * NG + g + 1

        def ticks(p, body, g):
            return p * BODIES + body * (SLOTS // 2) + g // 2 + 1

        def pipeline(eng, p, step, tail):
            def one(body, g, prev=True, nxt=True):
                step(SLOTS * body + g, g % SLOTS, ticks(p, body, g), ticks(p, body, g - 1), ticks(p, body, g + 1), prev, nxt)

            one(0, 0, prev=False)
            with eng.Fori(0, (NG - 2) // SLOTS) as body:
                for g in range(1, SLOTS + 1):
                    one(body, g)
            last = NG - 1
            one(last // SLOTS, last % SLOTS, nxt=False)
            tail(last, last % SLOTS, ticks(p, 0, last))

        @block.sync
        def _(sp):
            def load(dst, src):
                sp.dma_start(dst, src).then_inc(loaded, 16)

            load(xN[:, 0:FULL, :], x[0:FULL * P, :].rearrange("(t p) d -> p t d", p=P))
            load(rowsI[:, :], dst_gm)
            load(dstI[:, :], dst_pm)
            for k, (name, half) in enumerate((("msg_W1", 0), ("att_W1", 0), ("msg_W1", 1), ("att_W1", 1))):
                load(wcat[:, k * D:(k + 1) * D], w[name][half * D:(half + 1) * D, :])
            for k, name in enumerate(("msg_b1", "att_b1")):
                load(tabA[:, 0, k * D:(k + 1) * D], w[name].rearrange("(a d) -> a d", a=1).broadcast_to([P, D]))
            for dst, name in ((msgW2, "msg_W2"), (updW2, "upd_W2"), (glbW, "glb_W"), (Wq, "Wq"), (Wk, "Wk"),
                              (Wv, "Wv"), (Wl, "Wl")):
                load(dst[:, :], w[name])
            load(updW1[:, :, :], w["upd_W1"].rearrange("(a k) n -> k a n", a=2))
            load(attw[:, :], w["att_W2"].rearrange("d a -> a d").broadcast_to([P, D]))
            load(attb[:, :], w["att_b2"].rearrange("(a d) -> a d", a=1).broadcast_to([P, 1]))
            load(bvl[:, :], w["bl"].rearrange("(a d) -> a d", a=1).broadcast_to([P, D]))
            load(WkTb[:, D:D + 1], w["bk"].rearrange("(p a) -> p a", a=1))
            for k, name in ((UB1, "upd_b1"), (UB2, "upd_b2"), (GLB, "glb_b"), (BQ, "bq"), (BV, "bv"), (B2, "msg_b2")):
                load(col(k), w[name].rearrange("(p a) -> p a", a=1))
            sp.wait_ge(const_done, 1)
            sp.nop(nofuse=True)
            sp.dma_start(xN[0:REST, FULL, :], x[FULL * P:N, :]).then_inc(loaded_tail, 16)
            for s in a_out + b_out + x_out:
                sp.sem_inc(s, 16)
            for u in range(2):
                sp.sem_inc(out_sem[u], 64)
            R = rounds(sp)

            def one_pass(p, win, tab):
                sp.wait_ge(base_ready, p + 1)
                sp.nop(nofuse=True)

                width = win.shape[2]

                def step(g, u, ticks):
                    if ticks is not None:
                        for q in range(PAIRS):
                            sp.wait_ge(gathered[u][q], ticks * 32)
                            sp.nop(nofuse=True)
                    sp.dma_start(idx_st[:, u, :], idx[bass.ds(g * P, P), :]).then_inc(idx_ld[u], 16)
                    row = window(sp, g)
                    if ticks is not None:
                        sp.wait_ge(picked[u][PAIRS - 1], ticks)
                        sp.nop(nofuse=True)
                    for k in range(3):
                        sp.dma_start(win[k * WIN:(k + 1) * WIN, u, :],
                                     tab[bass.ds(row, WIN), k * width:(k + 1) * width]).then_inc(win_ld[u], 16)

                step(0, 0, None)
                step(1, 1, None)
                with sp.Fori(1, BODIES) as j:
                    step(2 * j, 0, p * BODIES + j)
                    step(2 * j + 1, 1, p * BODIES + j)

            def store_tables(q, rows, parts, parts_n):
                def store(tiles):
                    for tile, w, u, n, m in tiles:
                        at = bass.ds(tile * P, P)
                        if rows is not None:
                            sp.wait_ge(a_copied[u], n)
                            sp.nop(nofuse=True)
                            sp.dma_start(rows[at, :], tabA[:, w, :]).then_inc(a_out[w], 16)
                        sp.wait_ge(lo_done[u], n)
                        sp.nop(nofuse=True)
                        sp.dma_start(parts[at, :].rearrange("p (k d) -> p k d", k=3),
                                     tabB[:, w, :, 0:parts_n]).then_inc(b_out[w], 16)

                table_loop(sp, q, store)
                for w in range(4):
                    sp.wait_ge(b_out[w], (q + 1) * (uses(w) * 16) + 16)
                    sp.nop(nofuse=True)

            with sp.Fori(0, LAYERS) as l:
                store_tables(l, A_tab, B_tab, 2 * D)
                with sp.Fori(0, R) as r:
                    one_pass(l * R + r, bwin, B_tab)
            def rows_of(tab, c):
                return tab[bass.ds(c * CH, CH), :].rearrange("(k p) d -> p k d", k=4)

            with sp.Fori(0, CB) as b:
                for u in range(2):
                    sp.wait_ge(n_x1[u], b + 1)
                    sp.nop(nofuse=True)
                    sp.dma_start(rows_of(X_tab, 2 * b + u), outn[:, u, :, :]).then_inc(x_out[u], 16)
            store_tables(LAYERS, None, Q_tab, D + 1)
            with sp.Fori(0, R) as r:
                one_pass(LAYERS * R + r, qwin, Q_tab)

            def load_x1(c, u):
                sp.dma_start(x1n[:, u, :, :], rows_of(X_tab, c)).then_inc(x1_ld[u], 16)

            def store_out(c, u, n, known):
                sp.wait_ge(n_x1[u], n)
                sp.nop(nofuse=True)
                for k in range(4):
                    m = PIECE if known is None else min(PIECE, N - known * CH - k * PIECE)
                    if m > 0:
                        at = c * CH + k * PIECE
                        rows = bass.ds(at, PIECE) if known is None else slice(at, at + m)
                        sp.dma_start(out[rows, :], outn[0:m, u, k, :]).then_inc(out_sem[u], 16)

            for u in range(2):
                sp.wait_ge(x_out[u], CB * 16 + 16)
                sp.nop(nofuse=True)
                load_x1(u, u)
            with sp.Fori(0, CB - 1) as b:
                for u in range(2):
                    sp.wait_ge(n_c[u], b + 1)
                    sp.nop(nofuse=True)
                    load_x1(2 * b + u + 2, u)
                for u in range(2):
                    store_out(2 * b + u, u, CB + b + 1, None)
            for u in range(2):
                store_out(2 * (CB - 1) + u, u, 2 * CB, 2 * (CB - 1) + u)
            for u in range(2):
                pieces = sum(min(4, max(0, -(-(N - c * CH) // PIECE))) for c in range(u, 2 * CB, 2))
                sp.wait_ge(out_sem[u], 64 + 16 * pieces)
                sp.nop(nofuse=True)

        @block.gpsimd
        def _(pool):
            nc.gpsimd.memset(ident[:, :], 0.0).then_inc(ident_done, 1)
            nc.gpsimd.iota(iota_w[:, :, :], pattern=[[0, 3], [1, WIN]], base=0, channel_multiplier=0,
                           allow_small_or_imprecise_dtypes=True).then_inc(ident_done, 1)
            nc.gpsimd.iota(steps[:, :], pattern=[[WIN, ROUNDS]], base=0, channel_multiplier=0,
                           allow_small_or_imprecise_dtypes=True).then_inc(ident_done, 1)
            pool.wait_ge(ident_done, 3)
            pool.nop(nofuse=True)
            nc.gpsimd.affine_select(out=ident[:, :], in_=ident[:, :], compare_op=ALU.not_equal, fill=1.0,
                                    base=0, pattern=[[-1, P]], channel_multiplier=1).then_inc(ident_done, 1)
            R = rounds(pool)

            def wait_for_table(q):
                for w in range(4):
                    pool.wait_ge(a_out[w], (q + 1) * (uses(w) * 16) + 16)
                    pool.nop(nofuse=True)

            def fetch(u, t, row, tab):
                nc.gpsimd.indirect_dma_start(
                    row, None, tab,
                    bass.IndirectOffsetOnAxis(ap=idx_st[:, u, t:t + 1], axis=0)).then_inc(gathered[u][t // 2], 16)

            def gather_a(p):
                with pool.Fori(0, BODIES) as j:
                    n = p * BODIES + j + 1
                    for u in range(2):
                        pool.wait_ge(idx_ld[u], n * 16)
                        pool.nop(nofuse=True)
                        for t in range(TG):
                            if t % 2 == 0:
                                pool.wait_ge(added[u][t // 2], n)
                                pool.nop(nofuse=True)
                            fetch(u, t, arow[:, u, t, :], A_tab)

            def gather_x(p):
                def group(s, n):
                    u = s % 2
                    pool.wait_ge(idx_ld[u], n * 16)
                    pool.nop(nofuse=True)
                    pool.wait_ge(summed[u], n)
                    pool.nop(nofuse=True)
                    for t in range(TG):
                        fetch(u, t, xrow[:, s, t, 0:D], X_tab)

                with pool.Fori(0, NG // SLOTS) as body:
                    for g in range(SLOTS):
                        group(g, ticks(p, body, g))
                for g in range(NG // SLOTS * SLOTS, NG):
                    group(g % SLOTS, ticks(p, 0, g))

            with pool.Fori(0, LAYERS) as l:
                pool.wait_ge(u_h[1], l * CB + 1)
                pool.nop(nofuse=True)
                nc.gpsimd.memset(acc[:, :, :], 0.0).then_inc(acc_zero, 1)
                wait_for_table(l)
                with pool.Fori(0, R) as r:
                    gather_a(l * R + r)
            pool.wait_ge(u_h[1], LAYERS * CB + 1)
            pool.nop(nofuse=True)
            nc.gpsimd.memset(acc[:, :, :], 0.0).then_inc(acc_zero, 1)
            nc.gpsimd.memset(mrun[:, :], -BIG / 2).then_inc(acc_zero, 1)
            nc.gpsimd.memset(xrow[:, :, :, D:D + 1], 1.0).then_inc(acc_zero, 1)
            for u in range(2):
                pool.wait_ge(x_out[u], CB * 16 + 16)
                pool.nop(nofuse=True)
            with pool.Fori(0, R) as r:
                gather_x(LAYERS * R + r)

        @block.scalar
        def _(act):
            for k, first in enumerate(GROUPS4):
                m = min(4, NT - first)
                act.wait_ge(xt_ps, k + 1)
                act.nop(nofuse=True)
                nc.scalar.copy(xT[:, first * P:(first + m) * P], bank[k % 2][:, 0:m * P]).then_inc(xt_done, 1)
            act.wait_ge(setup_pe, 3)
            act.nop(nofuse=True)
            nc.scalar.activation(col(GH), bank[3][:, 0:1], ACT.Relu, bias=col(GLB)).then_inc(setup_act, 1)
            R = rounds(act)

            def tables(q, width, b_at, with_rows):
                def stage_tile(tile, u):
                    nc.scalar.copy(stage[:, u, :], hT[:, bass.ds(tile * P, P)]).then_inc(staged[u], 1)

                def copies(tiles):
                    for tile, w, u, n, m in tiles:
                        act.wait_ge(tab_ps[u], n)
                        act.nop(nofuse=True)
                        if with_rows:
                            act.wait_ge(a_out[w], m * 16)
                            act.nop(nofuse=True)
                            nc.scalar.copy(tabA[:, w, :], bank[w][:, 0:2 * D]).then_inc(a_copied[u], 1)
                        act.wait_ge(b_out[w], m * 16)
                        act.nop(nofuse=True)
                        nc.scalar.copy(tabB[:, w, 0, 0:width], bank[w][:, b_at:b_at + width]).then_inc(hi_done[u], 1)
                        if len(tiles) == 4:
                            stage_tile(tile + 2, u)

                for u in range(2):
                    stage_tile(u, u)
                table_loop(act, q, copies)

            def transposed(u, n, masked):
                act.wait_ge(ohp_ready[u], n)
                act.nop(nofuse=True)
                for h in range(2):
                    part = slice(h * 512, (h + 1) * 512)
                    nc.scalar.copy(oht[:, u, part], ohp[u][0:3 * WIN, part]).then_inc(oht_ready[u][h], 1)
                if masked:
                    nc.scalar.activation(mask[:, u, :], ohp[u][0:WIN, :], ACT.Copy, scale=BIG / 2, bias=-BIG / 2
                                         ).then_inc(mask_ready, 1)

            def sums_out(u, n):
                act.wait_ge(summed[u], n + SLOTS // 2)
                act.nop(nofuse=True)
                nc.scalar.copy(ssum[:, u, :], scat[u][0:WIN, 0:D + 1]).then_inc(sum_out[u], 1)

            def message_pass(p):
                def step(g, s, n, m, k, prev, nxt):
                    u = s % 2
                    for q in range(PAIRS):
                        two = slice(2 * q, 2 * q + 2)
                        act.wait_ge(added[u][q], n + 1)
                        act.nop(nofuse=True)
                        nc.scalar.activation(relu[:, u, two, 0:D], pre[:, u, two, 0:D], ACT.Relu)
                        if q == PAIRS - 1 and prev:
                            sums_out(1 - u, m)
                    if nxt:
                        transposed(1 - u, k, False)
                    act.wait_ge(dotted[u][PAIRS - 1], n)
                    act.nop(nofuse=True)
                    nc.scalar.activation(wt[:, u, :], lg[:, u, :], ACT.Sigmoid, bias=attb[:, :]).then_inc(wt_ready[u], 1)

                transposed(0, ticks(p, 0, 0), False)
                pipeline(act, p, step, lambda g, s, n: sums_out(s % 2, n))

            def update(l):
                with act.Fori(0, CB) as b:
                    n = l * CB + b + 1
                    for u in range(2):
                        act.wait_ge(u_pre[u], n)
                        act.nop(nofuse=True)
                        nc.scalar.activation(hid[:, u, :], t1[:, u, :], ACT.Relu, bias=col(UB1)).then_inc(u_relu[u], 1)

            with act.Fori(0, LAYERS) as l:
                act.wait_ge(u_h[1], l * CB + 1)
                act.nop(nofuse=True)
                tables(l, 2 * D, 2 * D, True)
                with act.Fori(0, R) as r:
                    message_pass(l * R + r)
                update(l)

            def load_sqrt():
                nc.scalar.activation(unused[:, :], eps_c[:, :], ACT.Sqrt)

            def norm(q):
                for u in range(2):
                    act.wait_ge(n_var[u], q)
                    act.nop(nofuse=True)
                    nc.scalar.activation(ystd[:, u, :], yvar[:, u, :], ACT.Sqrt, scale=1.0 / D,
                                         bias=eps_c[0:PIECE, :]).then_inc(n_std[u], 1)

            with act.Fori(0, CB) as b:
                load_sqrt()
                for u in range(2):
                    act.wait_ge(n_rows[u], b + 1)
                    act.nop(nofuse=True)
                    nc.scalar.copy(yc[:, u, :, :], rows_ps[u]).then_inc(n_d[u], 1)
                norm(b + 1)
                for u in range(2):
                    act.wait_ge(n_turned[u], b + 1)
                    act.nop(nofuse=True)
                    nc.scalar.copy(chunk(hT, 2 * b + u), bank[2 + u][:, 0:CH]).then_inc(n_back[u], 1)
            for u in range(2):
                act.wait_ge(n_back[u], CB + 1)
                act.nop(nofuse=True)
            tables(LAYERS, D + 1, 0, False)

            def attention_pass(p, r):
                def step(g, s, n, m, k, prev, nxt):
                    u = s % 2
                    a = group_tick(r, g)
                    if nxt:
                        transposed(1 - u, k, True)
                    if prev:
                        sums_out(1 - u, m)
                    act.wait_ge(s_sub, a)
                    act.nop(nofuse=True)
                    nc.scalar.activation(wt[:, u, :], sm[:, :], ACT.Exp).then_inc(wt_ready[u], 1)
                    act.wait_ge(s_diff, a)
                    act.nop(nofuse=True)
                    nc.scalar.activation(ed[:, u, :, :], diff[:, :, :], ACT.Exp).then_inc(s_ed, 1)

                transposed(0, ticks(p, 0, 0), True)
                pipeline(act, p, step, lambda g, s, n: sums_out(s % 2, n))

            with act.Fori(0, R) as r:
                attention_pass(LAYERS * R + r, r)

            with act.Fori(0, CB) as b:
                act.wait_ge(n_std[1], CB + b)
                act.nop(nofuse=True)
                load_sqrt()
                norm(CB + b + 1)

        @block.vector
        def _(v):
            v_ = nc.vector

            def three_parts(parts, whole, rest, part, ticks):
                v_.tensor_copy(part[0], whole).then_inc(setup_dve, 1)
                v.wait_ge(setup_dve, ticks + 1)
                v.nop(nofuse=True)
                v_.tensor_scalar(parts[:, :], part[0], ident[:, 0:1], None, ALU.mult)
                v_.tensor_tensor(rest, whole, part[0], ALU.subtract).then_inc(setup_dve, 1)
                v.wait_ge(setup_dve, ticks + 2)
                v.nop(nofuse=True)
                v_.tensor_copy(part[1], rest).then_inc(setup_dve, 1)
                v.wait_ge(setup_dve, ticks + 3)
                v.nop(nofuse=True)
                v_.scalar_tensor_tensor(out=parts[:, :], in0=part[1], scalar=ident[:, 1:2], in1=parts[:, :],
                                        op0=ALU.mult, op1=ALU.add)
                v_.tensor_tensor(part[2], rest, part[1], ALU.subtract).then_inc(setup_dve, 1)
                v.wait_ge(setup_dve, ticks + 4)
                v.nop(nofuse=True)
                v_.scalar_tensor_tensor(out=parts[:, :], in0=part[2], scalar=ident[:, 2:3], in1=parts[:, :],
                                        op0=ALU.mult, op1=ALU.add).then_inc(setup_dve, 1)

            v_.memset(xN[:, FULL:NT, :], 0.0).then_inc(const_done, 1)
            v_.memset(ones16[:, :], 1.0)
            v_.memset(eps_c[:, :], EPS)
            v_.memset(relu[:, :, :, D:D + 1], 1.0).then_inc(const_done, 1)
            for s in (added[0] + added[1], res_done, res_done):
                for one in s:
                    v.sem_inc(one, 1)
            for u in range(2):
                v.sem_inc(summed[u], SLOTS // 2)
                v.sem_inc(n_back[u], 1)
            v.wait_ge(loaded, 16 * LOADS)
            v.nop(nofuse=True)
            v_.tensor_reduce(rmin[:, :], rowsI[:, :], AX.X, ALU.min).then_inc(setup_dve, 1)
            v_.tensor_reduce(rmax[:, :], rowsI[:, :], AX.X, ALU.max).then_inc(setup_dve, 1)
            v.wait_ge(setup_dve, 2)
            v.nop(nofuse=True)
            v_.tensor_tensor(span[:, :], rmax[:, :], rmin[:, :], ALU.subtract).then_inc(setup_dve, 1)
            v.wait_ge(setup_pe, 1)
            v.nop(nofuse=True)
            v_.tensor_copy(base0[:, :], bank[2][0:1, 0:NG])
            v_.tensor_reduce(spanm[:, :], bank[2][0:1, NG:2 * NG], AX.X, ALU.max).then_inc(setup_dve, 1)
            v_.tensor_tensor(dst0[:, :].rearrange("p (g t) -> p g t", t=TG),
                             dstI[:, :].rearrange("p (g t) -> p g t", t=TG),
                             bank[2][:, 2 * NG:3 * NG].unsqueeze(2).to_broadcast([P, NG, TG]), ALU.subtract)
            v.wait_ge(setup_dve, 4)
            v.nop(nofuse=True)
            v.wait_ge(ident_done, 4)
            v.nop(nofuse=True)
            v_.tensor_scalar(centre[:, :], ident[:, :], -1.0 / D, None, ALU.add)
            v_.tensor_copy(ident16[:, :], ident[:, :])
            v_.tensor_copy(iota16[:, :], iota_w[:, :, :].rearrange("p k n -> p (k n)"))
            v_.tensor_scalar(within[:, :], steps[:, :], spanm[:, :], None, ALU.is_le).then_inc(setup_dve, 1)
            v.wait_ge(setup_dve, 5)
            v.nop(nofuse=True)
            v_.reduce_sum(count[:, :], within[:, :], AX.X).then_inc(setup_dve, 1)
            v.wait_ge(setup_dve, 6)
            v.nop(nofuse=True)
            v_.tensor_copy(roundsI[:, :], count[:, :]).then_inc(ready_all, 1)
            v.wait_ge(setup_pe, 2)
            v.nop(nofuse=True)
            v_.tensor_copy(WkTb[:, 0:D], bank[3][:, P:2 * P])
            v_.tensor_copy(col(B2U), bank[3][:, 1:2])
            v_.tensor_copy(WqT[:, :], bank[4][:, 0:P])
            v_.tensor_copy(WvT[:, :], bank[4][:, P:2 * P])
            v_.tensor_copy(msgW2T[:, :], bank[3][:, 2 * P:3 * P]).then_inc(setup_dve, 1)
            three_parts(b1parts, tabA[:, 0, :], res[:, 0, :], [tabB[:, 0, k, :] for k in range(3)], 7)
            for k, first in enumerate(GROUPS4):
                m = min(4, NT - first)
                v.wait_ge(xt_done, k + 1)
                v.nop(nofuse=True)
                v_.tensor_copy(hT[:, first * P:(first + m) * P], xT[:, first * P:(first + m) * P])
            v_.reduce_sum(col(SUMX), xT[:, 0:N], AX.X).then_inc(setup_dve, 1)
            v.wait_ge(setup_dve, 13)
            v.nop(nofuse=True)
            v_.tensor_scalar(col(SUMX), col(SUMX), 1.0 / N, None, ALU.mult).then_inc(setup_dve, 1)
            v.wait_ge(setup_act, 1)
            v.nop(nofuse=True)
            v_.tensor_copy(msg_upd[:, :], bank[3][:, 3 * P:4 * P]).then_inc(u_h[0], 1)
            v_.tensor_tensor(gcol[:, :], col(GH), col(UB2), ALU.add).then_inc(u_h[1], 1)
            v_.tensor_copy(Wqk[:, :], bank[4][:, 2 * P:3 * P + 1])
            v_.tensor_copy(Wvl[:, :], bank[5][:, 0:D])
            v_.tensor_tensor(t1[:, 0, 0:D], bvl[:, :], bank[5][:, 2 * P + 1:3 * P + 1], ALU.add).then_inc(setup_dve, 1)
            v.wait_ge(setup_dve, 15)
            v.nop(nofuse=True)
            v_.tensor_scalar(bvl[:, :], t1[:, 0, 0:D], ident[:, 0:1], None, ALU.mult)
            three_parts(qk_parts, bank[5][:, P:2 * P + 1], t2[:, 0, 0:D + 1], [junk[:, k, :] for k in range(3)], 15)
            R = rounds(v)

            def split(q, width, b_at):
                def rest(tiles):
                    for pair in (tiles[0:2], tiles[2:4]):
                        for tile, w, u, n, m in pair:
                            v.wait_ge(hi_done[u], n)
                            v_.tensor_tensor(res[:, u, 0:width], bank[w][:, b_at:b_at + width], tabB[:, w, 0, 0:width],
                                             ALU.subtract).then_inc(res_done[u], 1)
                        for tile, w, u, n, m in pair:
                            v.wait_ge(res_done[u], n + 2)
                            v_.tensor_copy(tabB[:, w, 1, 0:width], res[:, u, 0:width]).then_inc(mid_done[u], 1)
                        for tile, w, u, n, m in pair:
                            v.wait_ge(mid_done[u], n)
                            v_.tensor_tensor(tabB[:, w, 2, 0:width], res[:, u, 0:width], tabB[:, w, 1, 0:width],
                                             ALU.subtract).then_inc(lo_done[u], 1)
                        for tile, w, u, n, m in pair:
                            v.wait_ge(lo_done[u], n)
                            v.nop(nofuse=True)

                table_loop(v, q, rest)

            def write_base():
                v_.tensor_scalar(baseI[:, :], baseF[:, :], float(NPAD - WIN), None, ALU.min).then_inc(base_ready, 1)

            def all_rounds(l, one_pass):
                t0 = l * (2 * R + 1)
                v_.tensor_copy(baseF[:, :], base0[:, :])
                v_.tensor_copy(dst_rel[:, :], dst0[:, :]).then_inc(moved, 1)
                v.wait_ge(moved, t0 + 1)
                v.nop(nofuse=True)
                with v.Fori(0, R) as r:
                    v_.tensor_copy(rel16[:, :], dst_rel[:, :]).then_inc(moved, 1)
                    write_base()
                    v.wait_ge(moved, t0 + 2 * r + 2)
                    v.nop(nofuse=True)
                    one_pass(r)
                    v_.tensor_scalar(baseF[:, :], baseF[:, :], float(WIN), None, ALU.add)
                    v_.tensor_scalar(dst_rel[:, :], dst_rel[:, :], float(-WIN), None, ALU.add).then_inc(moved, 1)
                    v.wait_ge(moved, t0 + 2 * r + 3)
                    v.nop(nofuse=True)

            def one_hot(g, u):
                rel = rel16[:, bass.ds(g * TG, TG)].unsqueeze(2).to_broadcast([P, TG, 3 * WIN])
                nodes = iota16[:, :].unsqueeze(1).to_broadcast([P, TG, 3 * WIN])
                v_.tensor_tensor(oh[:, u, :, :], nodes, rel,
                                 ALU.is_equal).then_inc(oh_ready[u], 1)

            def weigh(u, n):
                v.wait_ge(wt_ready[u], n)
                v_.tensor_tensor(ohw[:, u, :, :], oh[:, u, :, 0:WIN],
                                 wt[:, u, :].unsqueeze(2).to_broadcast([P, TG, WIN]), ALU.mult
                                 ).then_inc(ohw_ready[u], 1)

            def message_pass(p):
                def add(u, n, q):
                    v.wait_ge(picked[u][q], n)
                    v.wait_ge(gathered[u][q], n * 32)
                    v_.tensor_tensor(pre[:, u, 2 * q:2 * q + 2, :], arow[:, u, 2 * q:2 * q + 2, :], bg[q],
                                     ALU.add).then_inc(added[u][q], 1)

                def dot(u, n, q):
                    v.wait_ge(added[u][q], n + 1)
                    for t in (2 * q, 2 * q + 1):
                        ins = v_.scalar_tensor_tensor(out=junk[:, t, 0:D], in0=pre[:, u, t, D:2 * D], scalar=0.0,
                                                      in1=attw[:, :], op0=ALU.max, op1=ALU.mult,
                                                      accum_out=lg[:, u, t:t + 1])
                    ins.then_inc(dotted[u][q], 1)

                def merge(row, u, n):
                    v.wait_ge(scat_done[u], n)
                    at = acc[:, :, bass.ds(row, WIN)]
                    v_.tensor_tensor(at, at, sc_sum[u], ALU.add).then_inc(merged[u], 1)

                def step(g, s, n, m, k, prev, nxt):
                    u = s % 2
                    add(u, n, 0)
                    add(u, n, 1)
                    dot(u, n, 0)
                    add(u, n, 2)
                    add(u, n, 3)
                    if nxt:
                        if prev:
                            v.wait_ge(ohw_ready[1 - u], m)
                            v.nop(nofuse=True)
                        one_hot(g + 1, 1 - u)
                    dot(u, n, 1)
                    dot(u, n, 2)
                    dot(u, n, 3)
                    if prev:
                        merge(window(v, g - 1), 1 - u, m)
                    weigh(u, n)

                v.wait_ge(base_ready, p + 1)
                v.nop(nofuse=True)
                one_hot(0, 0)
                pipeline(v, p, step, lambda g, s, n: merge(window(v, g), s % 2, n))

            def update(l):
                with v.Fori(0, CB) as b:
                    n = l * CB + b + 1
                    for u in range(2):
                        v.wait_ge(u_lin[u], n)
                        v.nop(nofuse=True)
                        v_.scalar_tensor_tensor(out=t1[:, u, :], in0=acc[:, 1, bass.ds((2 * b + u) * CH, CH)],
                                                scalar=col(B2U), in1=bank[u][:, 0:CH], op0=ALU.mult, op1=ALU.add
                                                ).then_inc(u_pre[u], 1)
                    for u in range(2):
                        v.wait_ge(u_new[u], n)
                        v.nop(nofuse=True)
                        h = chunk(hT, 2 * b + u)
                        v_.scalar_tensor_tensor(out=h, in0=bank[4 + u][:, 0:CH], scalar=gcol[:, :], in1=h,
                                                op0=ALU.add, op1=ALU.add).then_inc(u_h[u], 1)

            with v.Fori(0, LAYERS) as l:
                split(l, 2 * D, 2 * D)
                v.wait_ge(acc_zero, l + 1)
                v.nop(nofuse=True)
                all_rounds(l, lambda r: message_pass(l * R + r))
                update(l)

            def norm(q, before_result):
                for u in range(2):
                    for k in range(4):
                        ins = v_.scalar_tensor_tensor(out=ysq[:, u, k, :], in0=yc[:, u, k, :], scalar=1.0,
                                                      in1=yc[:, u, k, :], op0=ALU.mult, op1=ALU.mult,
                                                      accum_out=yvar[:, u, k:k + 1])
                    ins.then_inc(n_var[u], 1)
                for u in range(2):
                    v.wait_ge(n_std[u], q)
                    v_.reciprocal(yinv[:, u, :], ystd[:, u, :]).then_inc(n_r[u], 1)
                for u in range(2):
                    v.wait_ge(n_r[u], q)
                    before_result(u)
                    v_.tensor_tensor(outn[:, u, :, :], yc[:, u, :, :], yinv[:, u, :].unsqueeze(2).to_broadcast([PIECE, 4, D]),
                                     ALU.mult).then_inc(n_x1[u], 1)
                v.wait_ge(n_x1[1], q)
                v.nop(nofuse=True)

            v.wait_ge(u_h[1], LAYERS * CB + 1)
            with v.Fori(0, CB) as b:
                def stored(u):
                    v.wait_ge(x_out[u], b * 16 + 16)
                    v.nop(nofuse=True)
                    v.wait_ge(n_back[u], b + 1)
                    v.nop(nofuse=True)

                for u in range(2):
                    v_.tensor_tensor(t1[:, u, :], chunk(hT, 2 * b + u), chunk(xT, 2 * b + u), ALU.add
                                     ).then_inc(n_y[u], 1)
                for u in range(2):
                    v.wait_ge(n_d[u], b + 1)
                norm(b + 1, stored)
            split(LAYERS, D + 1, 0)

            def attention_pass(p, r):
                def dot(s, n, q):
                    u = s % 2
                    v.wait_ge(picked[u][q], n)
                    v.wait_ge(gathered[u][q], n * 32)
                    for t in (2 * q, 2 * q + 1):
                        at = (t % 2) * 2 * D
                        ins = v_.scalar_tensor_tensor(out=junk[:, t, :], in0=bank[q % 2][:, at:at + D + 1], scalar=1.0,
                                                      in1=xrow[:, s, t, :], op0=ALU.mult, op1=ALU.mult,
                                                      accum_out=lg[:, u, t:t + 1])
                    ins.then_inc(dotted[u][q], 1)

                def node_max(u, n, a):
                    v.wait_ge(mask_ready, a)
                    v.nop(nofuse=True)
                    v.wait_ge(s_spread, a)
                    v.nop(nofuse=True)
                    v_.tensor_tensor_reduce(out=junkm[:, :], in0=score_ps, in1=mask[:, u, :], scale=1.0,
                                            scalar=-BIG / 2, op0=ALU.add, op1=ALU.max, accum_out=mloc[:, :]
                                            ).then_inc(s_max, 1)
                    v.wait_ge(s_max, a)
                    v_.tensor_copy(m3[:, 0:1], mloc[:, :]).then_inc(s_hi, 1)
                    v.wait_ge(s_hi, a)
                    v_.tensor_tensor(m3[:, 1:2], mloc[:, :], m3[:, 0:1], ALU.subtract)
                    v_.tensor_tensor(mres[:, :], mloc[:, :], m3[:, 0:1], ALU.subtract).then_inc(s_mid, 1)
                    v.wait_ge(s_mid, a)
                    v_.tensor_tensor(m3[:, 2:3], mres[:, :], m3[:, 1:2], ALU.subtract).then_inc(s_lo, 1)

                def less_max(u, a):
                    v.wait_ge(s_me, a)
                    v_.tensor_reduce(me[:, :], sc_me, AX.X, ALU.add).then_inc(s_mer, 1)
                    v.wait_ge(s_mer, a)
                    v_.tensor_tensor(sm[:, :], lg[:, u, :], me[:, :], ALU.subtract).then_inc(s_sub, 1)

                def merge_max(row, a, prev):
                    old = mrun[:, bass.ds(row, WIN)]
                    v_.tensor_tensor(mnew[:, :], sc_max, old, ALU.max).then_inc(s_mnew, 1)
                    v.wait_ge(s_mnew, a)
                    if prev:
                        v.wait_ge(s_ed, a - 1)
                    v_.tensor_tensor(diff[:, 0, :], old, mnew[:, :], ALU.subtract)
                    v_.tensor_tensor(diff[:, 1, :], sc_max, mnew[:, :], ALU.subtract).then_inc(s_diff, 1)

                def merge(row, u, n, a):
                    at = acc[:, :, bass.ds(row, WIN)]
                    v.wait_ge(s_ed, a)
                    v.wait_ge(scat_done[u], n)
                    v_.tensor_tensor(newsc[:, :, :], sc_sum[u], ed[:, u, 1:2, :].to_broadcast([P, 2, WIN]), ALU.mult)
                    v_.tensor_tensor(oldsc[:, :, :], at, ed[:, u, 0:1, :].to_broadcast([P, 2, WIN]), ALU.mult
                                     ).then_inc(s_scaled, 1)
                    v.wait_ge(s_scaled, a)
                    v_.tensor_tensor(at, newsc[:, :, :], oldsc[:, :, :], ALU.add).then_inc(merged[u], 1)

                def step(g, s, n, m, k, prev, nxt):
                    u = s % 2
                    a = group_tick(r, g)
                    dot(s, n, 0)
                    dot(s, n, 1)
                    if nxt:
                        if prev:
                            v.wait_ge(ohw_ready[1 - u], m)
                            v.nop(nofuse=True)
                        one_hot(g + 1, 1 - u)
                    dot(s, n, 2)
                    dot(s, n, 3)
                    if prev:
                        row_before = window(v, g - 1)
                    node_max(u, n, a)
                    row = window(v, g)
                    less_max(u, a)
                    merge_max(row, a, prev)
                    weigh(u, n)
                    v.wait_ge(s_diff, a)
                    v.nop(nofuse=True)
                    v_.tensor_copy(mrun[:, bass.ds(row, WIN)], mnew[:, :])
                    if prev:
                        merge(row_before, 1 - u, m, a - 1)

                def tail(g, s, n):
                    v.wait_ge(merged[1 - s % 2], n)
                    v.nop(nofuse=True)
                    merge(window(v, g), s % 2, n, group_tick(r, g))

                v.wait_ge(base_ready, p + 1)
                v.nop(nofuse=True)
                one_hot(0, 0)
                pipeline(v, p, step, tail)

            v.wait_ge(acc_zero, LAYERS + 3)
            v.nop(nofuse=True)
            all_rounds(LAYERS, lambda r: attention_pass(LAYERS * R + r, r))

            v.wait_ge(merged[1], (LAYERS + 1) * (R * BODIES))
            v.nop(nofuse=True)
            def select(b):
                for u in range(2):
                    v_.scalar_tensor_tensor(out=t1[:, u, :], in0=acc[:, 1, bass.ds((2 * b + u) * CH, CH)], scalar=0.0,
                                            in1=chunk(hT, 2 * b + u), op0=ALU.is_le, op1=ALU.mult).then_inc(f_kept[u], 1)
                    v_.scalar_tensor_tensor(out=t2[:, u, :], in0=acc[:, 1, bass.ds((2 * b + u) * CH, CH)], scalar=0.0,
                                            in1=acc[:, 1, bass.ds((2 * b + u) * CH, CH)], op0=ALU.is_le, op1=ALU.add)
                    v.wait_ge(f_kept[u], b + 1)
                    v_.tensor_tensor(t1[:, u, :], t1[:, u, :], acc[:, 0, bass.ds((2 * b + u) * CH, CH)], ALU.add
                                     ).then_inc(f_sel[u], 1)

            def last_phase(b, nxt):
                n = b + 1
                for u in range(2):
                    v.wait_ge(f_rows[u], n)
                    v_.reciprocal(winv[:, u, :], bank[2 + u][0:PIECE, 0:4]).then_inc(f_winv[u], 1)
                for u in range(2):
                    v.wait_ge(f_winv[u], n)
                    v_.tensor_tensor(ysq[:, u, :, :], rows_ps[u], winv[:, u, :].unsqueeze(2).to_broadcast([PIECE, 4, D]),
                                     ALU.mult).then_inc(f_mul[u], 1)
                if nxt:
                    select(b + 1)
                for u in range(2):
                    v.wait_ge(f_mul[u], n)
                    v.wait_ge(x1_ld[u], n * 16)
                    v.nop(nofuse=True)
                    for k in range(4):
                        ins = v_.scalar_tensor_tensor(out=x1n[:, u, k, :], in0=ysq[:, u, k, :], scalar=0.0,
                                                      in1=x1n[:, u, k, :], op0=ALU.max, op1=ALU.add,
                                                      accum_out=ysum[:, u, k:k + 1])
                    ins.then_inc(n_y[u], 1)
                for u in range(2):
                    v.wait_ge(n_y[u], CB + n)
                    v_.tensor_scalar(ymean[:, u, :], ysum[:, u, :], 1.0 / D, None, ALU.mult).then_inc(n_mu[u], 1)
                for u in range(2):
                    v.wait_ge(n_mu[u], n)
                    v_.tensor_tensor(yc[:, u, :, :], x1n[:, u, :, :], ymean[:, u, :].unsqueeze(2).to_broadcast([PIECE, 4, D]),
                                     ALU.subtract).then_inc(n_c[u], 1)
                for u in range(2):
                    v.wait_ge(n_c[u], n)
                    v.wait_ge(out_sem[u], n * 64)
                    v.nop(nofuse=True)
                norm(CB + n, lambda u: None)

            select(0)
            with v.Fori(0, CB - 1) as b:
                last_phase(b, True)
            last_phase(CB - 1, False)

        @block.tensor
        def _(pe):
            mm, tr = nc.tensor.matmul, nc.tensor.transpose
            pe.wait_ge(loaded, 16 * LOADS)
            pe.nop(nofuse=True)
            pe.wait_ge(ident_done, 4)
            pe.nop(nofuse=True)
            pe.wait_ge(const_done, 2)
            pe.nop(nofuse=True)
            pe.wait_ge(setup_dve, 3)
            pe.nop(nofuse=True)
            mm(bank[2][0:1, 0:NG], rmin[:, :], ident[0:NG, 0:NG], start=True, stop=True)
            mm(bank[2][0:1, NG:2 * NG], span[:, :], ident[0:NG, 0:NG], start=True, stop=True)
            mm(bank[2][:, 2 * NG:3 * NG], rmin[:, 0:1].to_broadcast([NG, P]), ident[0:NG, 0:NG],
               start=True, stop=True).then_inc(setup_pe, 1)
            tr(bank[3][:, P:2 * P], Wk[:, :], ident[:, :])
            mm(bank[3][:, 1:2], updW1[:, 1, :], col(B2), start=True, stop=True)
            tr(bank[4][:, 0:P], Wq[:, :], ident[:, :])
            tr(bank[4][:, P:2 * P], Wv[:, :], ident[:, :])
            tr(bank[3][:, 2 * P:3 * P], msgW2[:, :], ident[:, :]).then_inc(setup_pe, 1)
            pe.wait_ge(loaded_tail, 16)
            pe.nop(nofuse=True)
            for k, first in enumerate(GROUPS4):
                if k >= 2:
                    pe.wait_ge(xt_done, k - 1)
                    pe.nop(nofuse=True)
                for t in range(first, min(first + 4, NT)):
                    ins = tr(bank[k % 2][:, (t - first) * P:(t - first + 1) * P], xN[:, t, :], ident[:, :])
                ins.then_inc(xt_ps, 1)
            pe.wait_ge(setup_dve, 14)
            pe.nop(nofuse=True)
            mm(bank[3][:, 3 * P:4 * P], msgW2T[:, :], updW1[:, 1, :], start=True, stop=True)
            mm(bank[4][:, 2 * P:3 * P + 1], WqT[:, :], WkTb[:, :], start=True, stop=True)
            mm(bank[5][:, 0:D], WvT[:, :], Wl[:, :], start=True, stop=True)
            mm(bank[5][:, P:2 * P + 1], col(BQ).to_broadcast([P, P]), WkTb[:, :], start=True, stop=True)
            mm(bank[5][:, 2 * P + 1:3 * P + 1], col(BV).to_broadcast([P, P]), Wl[:, :], start=True, stop=True)
            mm(bank[3][:, 0:1], glbW[:, :], col(SUMX), start=True, stop=True).then_inc(setup_pe, 1)
            R = rounds(pe)

            def tables(q, product):
                def products(tiles):
                    for tile, w, u, n, m in tiles:
                        pe.wait_ge(staged[u], n)
                        pe.nop(nofuse=True)
                        pe.wait_ge(res_done[u], n)
                        pe.nop(nofuse=True)
                        product(w, u).then_inc(tab_ps[u], 1)

                table_loop(pe, q, products)

            def message_rows(w, u):
                mm(bank[w], stage[:, u, :], wcat[:, :], start=True, stop=False)
                return mm(bank[w][:, 2 * D:4 * D], ones16[:, :], b1parts[:, :], start=False, stop=True)

            def query_rows(w, u):
                mm(bank[w][:, 0:D + 1], stage[:, u, :], Wqk[:, :], start=True, stop=False)
                return mm(bank[w][:, 0:D + 1], ones16[:, :], qk_parts[:, :], start=False, stop=True)

            def turn(u, n):
                pe.wait_ge(oh_ready[u], n)
                pe.nop(nofuse=True)
                for t in range(TG):
                    ins = tr(ohp[u][0:3 * WIN, t * P:(t + 1) * P], oh[:, u, t, :], ident16[:, :])
                ins.then_inc(ohp_ready[u], 1)

            def pick(u, q, into, win, width):
                for t in (2 * q, 2 * q + 1):
                    at = (t % 2) * 2 * D
                    ins = mm(into[:, at:at + width], oht[:, u, t * P:(t + 1) * P], win[:, u, :], start=True, stop=True)
                return ins

            def scatter(u, n, rows, part):
                if part[0] == 0:
                    pe.wait_ge(ohw_ready[u], n)
                for t in part:
                    ins = mm(scat[u][0:WIN, 0:D + 1], ohw[:, u, t, :], rows[:, t, :], start=(t == 0), stop=(t == TG - 1))
                if part[-1] == TG - 1:
                    ins.then_inc(summed[u], 1)

            def turn_sums(u, n):
                pe.wait_ge(sum_out[u], n)
                pe.nop(nofuse=True)
                tr(sc_sum[u][:, 0, :], ssum[:, u, 0:D], ident[0:WIN, 0:WIN])
                tr(sc_sum[u][:, 1, :], ssum[:, u, D:D + 1].to_broadcast([WIN, P]), ident[0:WIN, 0:WIN]
                   ).then_inc(scat_done[u], 1)

            def message_pass(p):
                def rows(u, n, m, q):
                    if q == 0:
                        pe.wait_ge(win_ld[u], n * 48)
                        pe.nop(nofuse=True)
                    pe.wait_ge(oht_ready[u][q // 2], n)
                    pe.nop(nofuse=True)
                    pe.wait_ge(added[1 - u][q], m + 1)
                    pick(u, q, bank[q], bwin, 2 * D).then_inc(picked[u][q], 1)

                def step(g, s, n, m, k, prev, nxt):
                    u = s % 2
                    before = relu[:, 1 - u, :, :]
                    for q in range(PAIRS):
                        rows(u, n, m, q)
                    if prev:
                        scatter(1 - u, m, before, range(TG))
                        turn_sums(1 - u, m)
                    if nxt:
                        turn(1 - u, k)

                def tail(g, s, n):
                    scatter(s % 2, n, relu[:, s % 2, :, :], range(TG))
                    turn_sums(s % 2, n)

                turn(0, ticks(p, 0, 0))
                pipeline(pe, p, step, tail)

            def update(l):
                pe.wait_ge(merged[1], (l + 1) * (R * BODIES))
                pe.nop(nofuse=True)
                with pe.Fori(0, CB) as b:
                    n = l * CB + b + 1
                    for u in range(2):
                        at = bass.ds((2 * b + u) * CH, CH)
                        mm(bank[u][:, 0:CH], updW1[:, 0, :], hT[:, at], start=True, stop=False)
                        mm(bank[u][:, 0:CH], msg_upd[:, :], acc[:, 0, at], start=False, stop=True).then_inc(u_lin[u], 1)
                    for u in range(2):
                        pe.wait_ge(u_relu[u], n)
                        pe.nop(nofuse=True)
                        pe.wait_ge(u_h[u], n)
                        pe.nop(nofuse=True)
                        mm(bank[4 + u][:, 0:CH], updW2[:, :], hid[:, u, :], start=True, stop=True
                           ).then_inc(u_new[u], 1)

            with pe.Fori(0, LAYERS) as l:
                tables(l, message_rows)
                with pe.Fori(0, R) as r:
                    message_pass(l * R + r)
                update(l)

            with pe.Fori(0, CB) as b:
                n = b + 1
                for u in range(2):
                    pe.wait_ge(n_y[u], n)
                    pe.nop(nofuse=True)
                    for k in range(4):
                        ins = mm(rows_ps[u][:, k, :], t1[:, u, k * PIECE:(k + 1) * PIECE], centre[:, :],
                                 start=True, stop=True)
                    ins.then_inc(n_rows[u], 1)
                for u in range(2):
                    pe.wait_ge(n_x1[u], n)
                    pe.nop(nofuse=True)
                    pe.wait_ge(n_back[u], n)
                    pe.nop(nofuse=True)
                    for k in range(4):
                        ins = tr(bank[2 + u][:, k * PIECE:(k + 1) * PIECE], outn[:, u, k, :], ident[0:PIECE, 0:PIECE])
                    ins.then_inc(n_turned[u], 1)
            tables(LAYERS, query_rows)

            def attention_pass(p, r):
                def rows(u, n, q):
                    if q == 0:
                        pe.wait_ge(win_ld[u], n * 48)
                        pe.nop(nofuse=True)
                    if q >= 2:
                        pe.wait_ge(dotted[u][q - 2], n)
                        pe.nop(nofuse=True)
                    pe.wait_ge(oht_ready[u][q // 2], n)
                    pe.nop(nofuse=True)
                    pick(u, q, bank[q % 2], qwin, D + 1).then_inc(picked[u][q], 1)

                def spread(u, n, q):
                    pe.wait_ge(dotted[u][q], n)
                    pe.nop(nofuse=True)
                    for t in (2 * q, 2 * q + 1):
                        ins = tr(score_ps[:, t * P:(t + 1) * P], lg[:, u, t:t + 1].to_broadcast([P, WIN]), ident[:, :])
                    return ins

                def step(g, s, n, m, k, prev, nxt):
                    u = s % 2
                    a = group_tick(r, g)
                    before = xrow[:, (s - 1) % SLOTS, :, :]
                    rows(u, n, 0)
                    rows(u, n, 1)
                    if prev:
                        scatter(1 - u, m, before, range(0, 4))
                    spread(u, n, 0)
                    rows(u, n, 2)
                    spread(u, n, 1)
                    rows(u, n, 3)
                    spread(u, n, 2)
                    spread(u, n, 3).then_inc(s_spread, 1)
                    if nxt:
                        turn(1 - u, k)
                    if prev:
                        scatter(1 - u, m, before, range(4, 8))
                    pe.wait_ge(s_lo, a)
                    pe.nop(nofuse=True)
                    for t in range(TG):
                        mm(sc_me[:, t, :], oht[0:WIN, u, t * P:(t + 1) * P], m3[:, :], start=True, stop=True)
                    tr(sc_max, mloc[:, 0:1].to_broadcast([WIN, P]), ident[0:WIN, 0:WIN]).then_inc(s_me, 1)
                    if prev:
                        turn_sums(1 - u, m)

                def tail(g, s, n):
                    scatter(s % 2, n, xrow[:, s, :, :], range(TG))
                    turn_sums(s % 2, n)

                turn(0, ticks(p, 0, 0))
                pipeline(pe, p, step, tail)

            with pe.Fori(0, R) as r:
                attention_pass(LAYERS * R + r, r)

            with pe.Fori(0, CB) as b:
                n = b + 1
                for u in range(2):
                    pe.wait_ge(f_sel[u], n)
                    pe.nop(nofuse=True)
                    for k in range(4):
                        piece = slice(k * PIECE, (k + 1) * PIECE)
                        mm(rows_ps[u][:, k, :], t1[:, u, piece], Wvl[:, :], start=True, stop=False)
                        mm(rows_ps[u][:, k, :], t2[:, u, piece], bvl[:, :], start=False, stop=True)
                        ins = mm(bank[2 + u][0:PIECE, k:k + 1], t2[:, u, piece], ident[:, 0:1], start=True, stop=True)
                    ins.then_inc(f_rows[u], 1)


_GNN = ("msg_W1", "msg_b1", "msg_W2", "msg_b2", "upd_W1", "upd_b1", "upd_W2", "upd_b2",
        "att_W1", "att_b1", "att_W2", "att_b2", "glb_W", "glb_b")
_ATT = ("Wq", "bq", "Wk", "bk", "Wv", "bv", "Wl", "bl")


def kernel(**inputs):
    import concourse.bacc as bacc
    from concourse.bass_utils import run_bass_kernel_spmd

    def padded(name, fill):
        a = np.full((NG * TG * P,), fill, np.int32)
        a[:E] = np.asarray(inputs[name])
        return a.reshape(NG, TG, P)

    src, dst = padded("src", 0), padded("dst", N)
    arrays = {
        "x": np.ascontiguousarray(inputs["x"]),
        "idx": np.ascontiguousarray(src.transpose(0, 2, 1)).reshape(NG * P, TG),
        "dst_pm": np.ascontiguousarray(dst.transpose(2, 0, 1)).reshape(P, NG * TG),
        "dst_gm": dst.reshape(NG, TG * P),
    }
    for prefix, names in (("L0_gnn_", _GNN), ("L1_gnn_", _ATT)):
        for n in names:
            arrays[n] = np.ascontiguousarray(inputs[prefix + n])
    nc = bacc.Bacc("TRN2", target_bir_lowering=False, num_devices=1)
    aps = {n: nc.dram_tensor(f"in_{n}", a.shape, mybir.dt.from_np(a.dtype), kind="ExternalInput").ap()
           for n, a in arrays.items()}
    out = nc.dram_tensor("out_0", (N, D), F32, kind="ExternalOutput").ap()
    build(nc, aps["x"], aps["idx"], aps["dst_pm"], aps["dst_gm"], aps, out)
    r = run_bass_kernel_spmd(nc, [{f"in_{n}": a for n, a in arrays.items()}], core_ids=[0])
    return r.results[0]["out_0"]
```
